# Optimizing a Trainium2 kernel written in Bass

```python
import numpy as np
import jax
import jax.numpy as jnp

def _softmax(x, axis=-1):
    return jax.nn.softmax(x, axis=axis)

def _gelu(x):
    return jax.nn.gelu(x, approximate=True)

def _silu(x):
    return jax.nn.silu(x)

def _sigmoid(x):
    return jax.nn.sigmoid(x)

def _layernorm(x, axis=-1, eps=1e-05):
    m = jnp.mean(x, axis=axis, keepdims=True)
    v = jnp.var(x, axis=axis, keepdims=True)
    return (x - m) / jnp.sqrt(v + eps)

def _scatter_add(tgt, idx, src, axis=0):
    return tgt.at[idx].add(src)

def _segment_sum(src, seg, n):
    return jax.ops.segment_sum(src, seg, n)
kernel_name = 'mk_xattn_ffn_d1_seqx_r2_e29240'

def setup_inputs(seed: int=0):
    np.random.seed(seed)
    _w = jnp.asarray

    def _rec_inputs():
        import jax
        import jax.numpy as jnp
        _rk = jax.random.key(seed)
        x = 7.22e-05 + 1 * jax.random.normal(jax.random.fold_in(_rk, 1), (16, 224, 512), jnp.float32)
        _lenS = 224 - jax.random.randint(jax.random.fold_in(_rk, 7), (16,), 0, max(1, 224 // 4) + 1, jnp.int32)
        _lenS2 = 750 - jax.random.randint(jax.random.fold_in(_rk, 8), (16,), 0, max(1, 750 // 4) + 1, jnp.int32)
        _ctx_1024P = jax.random.normal(jax.random.fold_in(_rk, 11), (16, 16, 512), jnp.float32)
        _ctx_1024c = jax.random.dirichlet(jax.random.fold_in(_rk, 511), 0.3 * jnp.ones((16,), jnp.float32), (16, 750))
        _ctx_1024t = jnp.einsum('bsk,bkd->bsd', _ctx_1024c, _ctx_1024P)
        _ctx_1024t = _ctx_1024t * jax.lax.rsqrt(jnp.mean(jnp.square(_ctx_1024t)) + 1e-12) * 0.953939
        ctx_1024 = 4.13588e-05 + 0.999923 * (_ctx_1024t + 0.3 * jax.random.normal(jax.random.fold_in(_rk, 611), (16, 750, 512), jnp.float32))
        return (x, ctx_1024)
    x, ctx_1024 = _rec_inputs()

    def _L0_xattn_setup():
        import jax, jax.numpy as jnp
        import numpy as np
        import math
        N_HEADS = 16
        D_MODEL = 512
        D_K = D_MODEL // N_HEADS
        key = jax.random.key(seed)
        ks = jax.random.split(key, 11)
        B, S = (4, 1024)
        scale = 1.0 / math.sqrt(D_MODEL)
        return {'q': jax.random.normal(ks[0], (B, S, D_MODEL), jnp.float32), 'k': jax.random.normal(ks[1], (B, S, D_MODEL), jnp.float32), 'v': jax.random.normal(ks[2], (B, S, D_MODEL), jnp.float32), 'Wq': jax.random.normal(ks[3], (D_MODEL, D_MODEL), jnp.float32) * scale, 'bq': jax.random.normal(ks[4], (D_MODEL,), jnp.float32) * 0.01, 'Wk': jax.random.normal(ks[5], (D_MODEL, D_MODEL), jnp.float32) * scale, 'bk': jax.random.normal(ks[6], (D_MODEL,), jnp.float32) * 0.01, 'Wv': jax.random.normal(ks[7], (D_MODEL, D_MODEL), jnp.float32) * scale, 'bv': jax.random.normal(ks[8], (D_MODEL,), jnp.float32) * 0.01, 'Wo': jax.random.normal(ks[9], (D_MODEL, D_MODEL), jnp.float32) * scale, 'bo': jax.random.normal(ks[10], (D_MODEL,), jnp.float32) * 0.01}
    _L0_xattn_all = _L0_xattn_setup()
    _L0_xattn_in = {k: v for k, v in _L0_xattn_all.items() if k in ('Wq', 'bq', 'Wk', 'bk', 'Wv', 'bv', 'Wo', 'bo')}
    del _L0_xattn_all

    def _L0_ffn_setup():
        import jax, jax.numpy as jnp
        import numpy as np
        BLOCK = 16
        _GRID = jnp.array([0.0, 0.5, 1.0, 1.5, 2.0, 3.0, 4.0, 6.0], dtype=jnp.float32)
        _MID = jnp.array([0.25, 0.75, 1.25, 1.75, 2.5, 3.5, 5.0], dtype=jnp.float32)

        def fp4_quant_dequant(x):
            shape = x.shape
            xb = x.reshape(shape[:-1] + (shape[-1] // BLOCK, BLOCK))
            scale = jnp.max(jnp.abs(xb), axis=-1, keepdims=True) / 6.0
            scale = jnp.maximum(scale, jnp.float32(1e-12))
            xn = xb / scale
            idx = jnp.searchsorted(_MID, jnp.abs(xn))
            q = _GRID[idx] * jnp.sign(xn) * scale
            return q.reshape(shape)

        def fp4_linear(x, w):
            xq = fp4_quant_dequant(x)
            wq = fp4_quant_dequant(w)
            return jnp.einsum('bsk,nk->bsn', xq, wq)
        key = jax.random.key(seed)
        k1, k2, k3, k4 = jax.random.split(key, 4)
        H, I = (512, 1408)
        x = jax.random.normal(k1, (4, 2048, H), dtype=jnp.float32)
        w_gate = jax.random.normal(k2, (I, H), dtype=jnp.float32) * 0.02
        w_up = jax.random.normal(k3, (I, H), dtype=jnp.float32) * 0.02
        w_down = jax.random.normal(k4, (H, I), dtype=jnp.float32) * 0.02
        return {'x': x, 'w_gate': w_gate, 'w_up': w_up, 'w_down': w_down}
    _L0_ffn_all = _L0_ffn_setup()
    _L0_ffn_in = {k: v for k, v in _L0_ffn_all.items() if k in ('w_gate', 'w_up', 'w_down')}
    del _L0_ffn_all
    return {'x': x, 'ctx_1024': ctx_1024, 'L0_xattn_Wq': _L0_xattn_in['Wq'], 'L0_xattn_bq': _L0_xattn_in['bq'], 'L0_xattn_Wk': _L0_xattn_in['Wk'], 'L0_xattn_bk': _L0_xattn_in['bk'], 'L0_xattn_Wv': _L0_xattn_in['Wv'], 'L0_xattn_bv': _L0_xattn_in['bv'], 'L0_xattn_Wo': _L0_xattn_in['Wo'], 'L0_xattn_bo': _L0_xattn_in['bo'], 'L0_ffn_w_gate': _L0_ffn_in['w_gate'], 'L0_ffn_w_up': _L0_ffn_in['w_up'], 'L0_ffn_w_down': _L0_ffn_in['w_down']}

def reference(x, ctx_1024, L0_xattn_Wq, L0_xattn_bq, L0_xattn_Wk, L0_xattn_bk, L0_xattn_Wv, L0_xattn_bv, L0_xattn_Wo, L0_xattn_bo, L0_ffn_w_gate, L0_ffn_w_up, L0_ffn_w_down):
    import jax
    import jax.numpy as jnp

    def _L0_xattn_ref(q, k, v, Wq, bq, Wk, bk, Wv, bv, Wo, bo):
        import jax, jax.numpy as jnp
        import numpy as np
        import math
        N_HEADS = 16
        D_MODEL = 512
        D_K = D_MODEL // N_HEADS
        B, S, _ = q.shape

        def proj(x, W, b):
            y = x @ W.T + b
            return y.reshape(B, -1, N_HEADS, D_K).transpose(0, 2, 1, 3)
        qh = proj(q, Wq, bq)
        kh = proj(k, Wk, bk)
        vh = proj(v, Wv, bv)
        scores = jnp.einsum('bhqd,bhkd->bhqk', qh, kh) / math.sqrt(D_K)
        attn = jax.nn.softmax(scores, axis=-1)
        out = jnp.einsum('bhqk,bhkd->bhqd', attn, vh)
        concat = out.transpose(0, 2, 1, 3).reshape(B, -1, D_MODEL)
        return concat @ Wo.T + bo

    def _L0_ffn_ref(x, w_gate, w_up, w_down):
        import jax, jax.numpy as jnp
        import numpy as np
        BLOCK = 16
        _GRID = jnp.array([0.0, 0.5, 1.0, 1.5, 2.0, 3.0, 4.0, 6.0], dtype=jnp.float32)
        _MID = jnp.array([0.25, 0.75, 1.25, 1.75, 2.5, 3.5, 5.0], dtype=jnp.float32)

        def fp4_quant_dequant(x):
            shape = x.shape
            xb = x.reshape(shape[:-1] + (shape[-1] // BLOCK, BLOCK))
            scale = jnp.max(jnp.abs(xb), axis=-1, keepdims=True) / 6.0
            scale = jnp.maximum(scale, jnp.float32(1e-12))
            xn = xb / scale
            idx = jnp.searchsorted(_MID, jnp.abs(xn))
            q = _GRID[idx] * jnp.sign(xn) * scale
            return q.reshape(shape)

        def fp4_linear(x, w):
            xq = fp4_quant_dequant(x)
            wq = fp4_quant_dequant(w)
            return jnp.einsum('bsk,nk->bsn', xq, wq)
        gate = fp4_linear(x, w_gate)
        y = fp4_linear(x, w_up)
        h = jax.nn.silu(gate) * y
        return fp4_linear(h, w_down)
    x = x + _L0_xattn_ref(_layernorm(x, axis=-1), ctx_1024, ctx_1024, L0_xattn_Wq, L0_xattn_bq, L0_xattn_Wk, L0_xattn_bk, L0_xattn_Wv, L0_xattn_bv, L0_xattn_Wo, L0_xattn_bo)
    x = x + _L0_ffn_ref(_layernorm(x, axis=-1), L0_ffn_w_gate, L0_ffn_w_up, L0_ffn_w_down)
    return x

_drawn_inputs = setup_inputs


def setup_inputs(seed=0):
    import zlib

    import numpy as np

    out = dict(_drawn_inputs(seed))
    spreads = {}
    factors = {'L0_xattn_bq': 26.972, 'L0_xattn_bk': 64.0, 'L0_xattn_bv': 5.245, 'L0_xattn_bo': 4.932}
    for name, (base, spread) in spreads.items():
        noise = np.random.default_rng([zlib.crc32(name.encode()), seed]).standard_normal(out[name].shape)
        drawn = base * np.exp(spread * noise) if base else spread * noise
        out[name] = jnp.asarray(drawn.astype(out[name].dtype))
    for name, factor in factors.items():
        out[name] = (out[name] * factor).astype(out[name].dtype)
    return out
```

```python
import concourse.bass as bass
from concourse import mybir
from contextlib import ExitStack

F32 = mybir.dt.float32
F32R = mybir.dt.float32r
U32 = mybir.dt.uint32
ALU = mybir.AluOpType
ACT = mybir.ActivationFunctionType
AX = mybir.AxisListType

P = 128
D = 512
KC = D // P
DK = 32
HG = P // DK
NG = D // P
SQ = 224
QH = SQ // 2
SK = 750
KT = 6
KW = SK // KT
SKP = (KT - 1) * KW + P + 1
KSPLIT = (0, 376, SK)
SHIFT = 3 * DK
STK = SHIFT + HG
F = 1408
FC = F // P
CH = (0, 512, 1024, F)
BLK = 16
WU = 2 * FC + FC
EPS = 1e-5
PASSES = ((0, 0), (0, 1), (1, 0))
EXP_MASK = 0x7F800000
SIGN_MASK = 0x80000000
KEEP_MASK = 0xFFE00000
TIE = 2.25 - 2.0 ** -22
QSTEPS = 11


def reached(engine, sem, count):
    if not isinstance(count, int) or count > 0:
        engine.wait_ge(sem, count)


def attention_weights(nc, ctx, dram, w_hi_lo, consts):
    raw = [ctx.enter_context(nc.sbuf_tensor(f"w_raw{i}", [P, KC, D], F32)) for i in range(2)]
    loaded = [ctx.enter_context(nc.semaphore(f"w_loaded{i}")) for i in range(2)]
    small_loaded = ctx.enter_context(nc.semaphore("small_loaded"))
    hi_done = ctx.enter_context(nc.semaphore("w_hi_done"))
    lo_done = ctx.enter_context(nc.semaphore("w_lo_done"))
    zeroed = ctx.enter_context(nc.semaphore("consts_zeroed"))
    made = ctx.enter_context(nc.semaphore("consts_made"))
    pick = ctx.enter_context(nc.sbuf_tensor("pick", [STK, HG, SKP], F32))
    kstack, ctx_hi, ctx_lo, ident, ones, ln_consts, biases, bo_rows = consts
    block = ctx.enter_context(nc.Block())

    @block.sync
    def _(sp):
        for n, src in enumerate((dram["bq"], dram["bk"], dram["bv"])):
            sp.dma_start(biases[:, n, :], src).then_inc(small_loaded, 16)
        sp.dma_start(bo_rows[:, :], dram["bo"].partition_broadcast(QH)).then_inc(small_loaded, 16)
        for n, name in enumerate(("wq", "wk", "wv", "wo")):
            if n >= 2:
                sp.wait_ge(lo_done, n - 1)
            sp.dma_start(raw[n % 2][:, :, :], dram[name]).then_inc(loaded[n % 2], 16)
        sp.wait_ge(small_loaded, 64)

    @block.scalar
    def _(act):
        for n in range(4):
            act.wait_ge(loaded[n % 2], 16 * (n // 2 + 1))
            nc.scalar.activation(w_hi_lo[n][0][:, :, :], raw[n % 2][:, :, :], ACT.Copy).then_inc(hi_done, 1)
        act.wait_ge(made, 2)
        for par in range(2):
            nc.scalar.activation(kstack[par][SHIFT:STK, :, :], pick[SHIFT:STK, :, :], ACT.Copy)

    @block.vector
    def _(dve):
        nc.vector.memset(ones[:, :], 1.0)
        nc.vector.memset(ln_consts[:, 0:1], -0.5)
        nc.vector.memset(ln_consts[:, 1:2], EPS)
        for n in range(4):
            dve.wait_ge(hi_done, n + 1)
            nc.vector.tensor_tensor(w_hi_lo[n][1][:, :, :], raw[n % 2][:, :, :],
                                    w_hi_lo[n][0][:, :, :].bitcast(F32), ALU.subtract).then_inc(lo_done, 1)

    @block.gpsimd
    def _(pool):
        nc.gpsimd.memset(ident[:, :], 0.0).then_inc(zeroed, 1)
        for par in range(2):
            nc.gpsimd.memset(kstack[par][:, :, :].bitcast(F32), 0.0).then_inc(zeroed, 1)
        nc.gpsimd.memset(ctx_hi[:, :, SK:SKP].bitcast(F32), 0.0)
        nc.gpsimd.memset(ctx_lo[:, :, SK:SKP].bitcast(F32), 0.0).then_inc(zeroed, 1)
        pool.wait_ge(zeroed, 4)
        nc.gpsimd.memset(pick[SHIFT:STK, :, :], 0.0).then_inc(zeroed, 1)
        pool.wait_ge(zeroed, 5)
        nc.gpsimd.affine_select(out=ident[:, :], in_=ident[:, :], compare_op=ALU.not_equal, fill=1.0,
                                base=0, pattern=[[-1, P]], channel_multiplier=1).then_inc(made, 1)
        pool.wait_ge(made, 1)
        nc.gpsimd.affine_select(out=pick[SHIFT:STK, :, :], in_=pick[SHIFT:STK, :, :], compare_op=ALU.not_equal,
                                fill=1.0, base=0, pattern=[[-1, HG], [0, SKP]], channel_multiplier=1)\
            .then_inc(made, 1)


FFN_SLOTS = (0, 1, 3)
FFN_STEPS = ((), (), (), (1,), (2, 3), (4,), (5,), (6,), (7,), (8,), (9,), (10, 11))
MAX_STEPS = (2, 1, 2, 1, 2, 1, 2, 1, 2, 1, 1, 0)


def slot_units(g, first, last):
    units = []
    maxima = 0
    for i in range(12):
        p, j = i // 4, i % 4
        units.append(("score", g, p, j))
        if i == 0:
            if not (last and g == 3):
                units.append(("stack_low", g + 1))
            if g in FFN_SLOTS:
                units.append(("ffn_load", FFN_SLOTS.index(g)))
            if not (last and g == 3):
                units.append(("stack", g + 1))
        if not (first and g == 0):
            if i == 1:
                units.append(("pv", g - 1, 2))
            if i == 8:
                units += [("sum", g - 1)]
            if i == 10:
                units += [("sum_lo", g - 1)]
        if i in (5, 9):
            units.append(("pv", g, i // 4 - 1))
        if not (last and g == 3):
            for _ in range(MAX_STEPS[i]):
                units.append(("max", g + 1, maxima))
                maxima += 1
            if i in (7, 11):
                units.append(("shift", g + 1, i // 8))
        if g in FFN_SLOTS:
            m = FFN_SLOTS.index(g)
            units += [("ffn_quant", m, n) for n in FFN_STEPS[i]]
            if i == 11:
                units.append(("ffn_store", m))
        if g == 1 and not first:
            if i in (2, 3):
                units.append(("out", -1, i - 2))
        if g == 2 and not last:
            if i < 4:
                units.append(("ctx", 1, i))
            if i in (2, 3):
                units.append(("xt", 1, i - 2))
            if i in (3, 4):
                units.append(("xt_lo", 1, i - 3))
        if g == 1 and not last:
            if i in (5, 6):
                units.append(("norm", 1, i - 5))
            if i in (8, 9):
                units.append(("norm2", 1, i - 8))
        if g == 0 and i == 2 and not last:
            units += [("load_ctx", 1), ("load_x", 1)]
        if g == 3 and i == 6:
            units.append(("load_res", 0))
        if g < 2 or not last:
            units += {4: [("k", g + 2, 0)], 5: [("k", g + 2, 1), ("k_lo", g + 2, 0)],
                      6: [("q", g + 2), ("k_lo", g + 2, 1)], 7: [("q_lo", g + 2)]}.get(i, [])
            if i in (8, 10, 11):
                half = 1 if g < 2 else 0
                units.append(("v", 0 if g < 2 else 1, half, 3 * (g % 2) + {8: 0, 10: 1, 11: 2}[i]))
    return units


def batch_units(first, last):
    return [u for g in range(NG) for u in slot_units(g, first, last)]


def start_units():
    units = [("load_ctx", 0), ("load_x", 0)]
    units += [("norm", 0, 0), ("norm", 0, 1), ("norm2", 0, 0), ("norm2", 0, 1)]
    units += [("ctx", 0, c) for c in range(KC)]
    units += [("xt", 0, 0), ("xt", 0, 1), ("xt_lo", 0, 0), ("xt_lo", 0, 1)]
    for t in range(2):
        units += [("k", t, 0), ("k", t, 1), ("k_lo", t, 0), ("q", t), ("k_lo", t, 1), ("q_lo", t)]
        if t == 0:
            units += [("stack_low", 0), ("stack", 0)]
    units += [("v", 0, 0, n) for n in range(KT)]
    return units + [(u[0], 0, u[2]) for u in slot_units(NG - 1, True, False) if u[0] in ("max", "shift")]


END_UNITS = [("pv", 3, 2), ("sum", 3), ("sum_lo", 3), ("out", 0, 0), ("out", 0, 1)]


def attention(nc, ctx, dram, w_hi_lo, consts, x1, ffn_raw, ffn_quant, batches):
    def sb(name, shape, dt=F32):
        return ctx.enter_context(nc.sbuf_tensor(name, shape, dt))

    def bank(name):
        return ctx.enter_context(nc.psum_tensor(name, [P, 512], F32))

    def sem(name):
        return ctx.enter_context(nc.semaphore(name))

    kstack, ctx_hi, ctx_lo, ident, ones, ln_consts, biases, bo_rows = consts
    ctx_raw = sb("ctx_raw", [P, KC, SK])
    ctx_part = (ctx_hi, ctx_lo)
    qstack = [sb(f"qstack{i}", [STK, HG, SQ], F32R) for i in range(2)]
    k_low = sb("k_low", [P, SK], F32R)
    k_part = [[sb(f"k_high{i}", [P, SK], F32R), k_low] for i in range(2)]
    q_part = [[sb(f"q_part{i}{h}", [P, SQ], F32R) for h in range(2)] for i in range(2)]
    values = sb("values", [KW, 2, KT, 256])
    probs = [sb(f"probs{p}", [KW, HG, 2, SQ]) for p in range(3)]
    prob_sum = sb("prob_sum", [KW, HG, SQ])
    heads = sb("heads", [P, SQ])
    o_part = [sb(f"o_part{h}", [P, NG, SQ], F32R) for h in range(2)]
    xn = sb("xn", [QH, 2, D])
    xt_part = [sb(f"xt_part{h}", [P, KC, SQ], F32R) for h in range(2)]
    res = sb("res", [QH, 2, D])
    share = F * D // (P * batches)
    fw_share, fw_power = sb("fw_share", [P, share]), sb("fw_power", [P, share])
    fw_scales = [sb(f"fw_{n}", [P, share // BLK]) for n in ("amax", "scale", "inv_scale")]
    stats = sb("stats", [QH, 2, 6])
    mean_var = sb("mean_var", [QH, 2, 2])
    rstd = sb("rstd", [QH, 2])
    spacer = sb("spacer", [P, 1])
    row_max = sb("row_max", [QH, 2, HG, 2])
    neg_max = sb("neg_max", [QH, 2, HG])

    score_bank = [bank(f"score_bank{i}") for i in range(2)]
    max_bank = [bank(f"max_bank{i}") for i in range(2)]
    proj_bank = [bank(f"proj_bank{i}") for i in range(2)]
    pv_bank = [bank(f"pv_bank{i}") for i in range(2)]

    names = ("score", "max", "shift", "k", "q", "v", "xt", "out", "pv", "sum")
    made = {n: sem(f"{n}_made") for n in names}
    exp_done = sem("exp_done")
    hi_done = {n: sem(f"{n}_hi_done") for n in ("k", "q", "xt", "ctx", "sum")}
    lo_done = {n: sem(f"{n}_lo_done") for n in ("k", "q", "xt", "ctx", "sum")}
    v_copied = sem("v_copied")
    shift_copied = sem("shift_copied")
    max_reduced = sem("max_reduced")
    max_negated = sem("max_negated")
    inverted = sem("sum_inverted")
    normalized = sem("heads_normalized")
    summed = sem("probs_summed")
    stats_done = sem("ln_stats")
    var_done = sem("ln_var")
    pow_steps = sem("ln_pow_steps")
    xn_done = sem("xn_done")
    bias_added = sem("res_bias_added")
    x1_done = sem("x1_done")
    ctx_loaded = sem("ctx_loaded")
    x_loaded = sem("x_loaded")
    res_loaded = sem("res_loaded")
    x1_stored = sem("x1_stored")
    stacked = [sem(f"stacked{i}") for i in range(2)]
    low_stacked = sem("low_stacked")
    fw_loaded = sem("fw_share_loaded")
    fw_steps = sem("fw_quant_steps")
    fw_stored = sem("fw_share_stored")
    STACK_DMAS = 5 * HG

    def index_of(unit, b):
        kind = unit[0]
        if kind == "v":
            return ((b + unit[1]) * 2 + unit[2]) * KT + unit[3]
        per = {"score": 12, "max": 16, "shift": 2, "k": 2, "q": 1, "pv": 3, "sum": 1}
        if kind in per:
            place = unit[2] * 4 + unit[3] if kind == "score" else unit[2] if len(unit) > 2 else 0
            return (b * NG + unit[1]) * per[kind] + place
        return (b + unit[1]) * {"xt": 2, "out": 2, "ctx": KC}[kind] + unit[2]

    def count(b, *unit):
        return index_of(unit, b) + 1

    def stack_count(b, t):
        return (b * (NG // 2) + t // 2 + 1) * 16 * STACK_DMAS

    def low_count(b, t):
        return (b * NG + t + 1) * 16 * HG

    def freed(engine, unit, b):
        kind = unit[0]
        done = {"k": lo_done["k"], "q": lo_done["q"], "xt": lo_done["xt"], "v": v_copied, "out": x1_done,
                "max": max_reduced, "shift": shift_copied}[kind]
        reached(engine, done, count(b, *unit))

    def phases(engine, body):
        body(0, start_units(), [None, None], [None, None])
        v_end = [("v", 0, 0, KT - 2), ("v", 0, 0, KT - 1)]
        m_end = [("max", 0, 15), ("shift", 0, 1)]
        body(0, batch_units(True, False), list(v_end), list(m_end))
        with engine.Fori(1, batches - 1) as b:
            body(b, batch_units(False, False), list(v_end), list(m_end))
        v_last = [("v", 0, 1, KT - 2), ("v", 0, 1, KT - 1)]
        body(batches - 1, batch_units(False, True), list(v_end), list(m_end))
        body(batches - 1, END_UNITS, v_last, [None, None])

    block = ctx.enter_context(nc.Block())

    @block.tensor
    def _(pe):
        def body(b, units, proj_last, max_last):
            proj = mx = 0
            for u in units:
                kind, t = u[0], u[1]
                if kind in ("k", "q", "v", "xt", "out"):
                    out = proj_bank[proj % 2]
                    if proj_last[proj % 2] is not None:
                        freed(pe, proj_last[proj % 2], b)
                    proj_last[proj % 2] = u
                    proj += 1
                if kind in ("max", "shift"):
                    out = max_bank[mx % 2]
                    if max_last[mx % 2] is not None:
                        freed(pe, max_last[mx % 2], b)
                    max_last[mx % 2] = u
                    mx += 1
                if kind == "k":
                    lo, hi = KSPLIT[u[2]], KSPLIT[u[2] + 1]
                    g = t % NG
                    if g == 0 and u[2] == 0:
                        reached(pe, lo_done["ctx"], count(b, "ctx", t // NG, KC - 1))
                    n = 0
                    for c in range(KC):
                        for ws, cs in PASSES:
                            last = nc.tensor.matmul(out[:, 0:hi - lo], w_hi_lo[1][ws][:, c, g * P:(g + 1) * P],
                                                    ctx_part[cs][:, c, lo:hi], start=(n == 0), stop=(n == 11))
                            n += 1
                    last.then_inc(made["k"], 1)
                elif kind == "q":
                    g = t % NG
                    if g == 0:
                        reached(pe, lo_done["xt"], count(b, "xt", t // NG, 1))
                    n = 0
                    for c in range(KC):
                        for ws, cs in PASSES:
                            last = nc.tensor.matmul(out[:, 0:SQ], w_hi_lo[0][ws][:, c, g * P:(g + 1) * P],
                                                    xt_part[cs][:, c, :], start=(n == 0), stop=(n == 11))
                            n += 1
                    last.then_inc(made["q"], 1)
                elif kind == "v":
                    half, kt = u[2], u[3]
                    n = 0
                    for c in range(KC):
                        for cs, ws in PASSES:
                            last = nc.tensor.matmul(out[:, 0:256], ctx_part[cs][:, c, kt * KW:kt * KW + P],
                                                    w_hi_lo[2][ws][:, c, half * 256:(half + 1) * 256],
                                                    start=(n == 0), stop=(n == 11))
                            n += 1
                    last.then_inc(made["v"], 1)
                elif kind == "xt":
                    reached(pe, xn_done, 2 * (b + t) + u[2] + 1)
                    for c in range(KC):
                        last = nc.tensor.transpose(out[:, c * QH:(c + 1) * QH], xn[:, u[2], c * P:(c + 1) * P],
                                                   ident[0:QH, 0:QH])
                    last.then_inc(made["xt"], 1)
                elif kind == "out":
                    reached(pe, lo_done["sum"], count(b, "sum", NG * t + 3))
                    n = 0
                    for g in range(NG):
                        for os_, ws in PASSES:
                            last = nc.tensor.matmul(out[0:QH, :], o_part[os_][:, g, u[2] * QH:(u[2] + 1) * QH],
                                                    w_hi_lo[3][ws][:, g, :], start=(n == 0), stop=(n == 11))
                            n += 1
                    last.then_inc(made["out"], 1)
                elif kind == "max":
                    half, j, kh = u[2] // 8, u[2] % 8 // 2, u[2] % 2
                    if u[2] == 0:
                        reached(pe, hi_done["k"], count(b, "k", t, 1))
                        reached(pe, hi_done["q"], count(b, "q", t))
                    lo, hi = KSPLIT[kh], KSPLIT[kh + 1]
                    rows = slice(j * DK, (j + 1) * DK)
                    nc.tensor.matmul(out[0:QH, 0:hi - lo], q_part[t % 2][0][rows, half * QH:(half + 1) * QH],
                                     k_part[t % 2][0][rows, lo:hi], start=True, stop=True).then_inc(made["max"], 1)
                elif kind == "shift":
                    reached(pe, max_negated, count(b, "shift", t, u[2]))
                    nc.tensor.matmul(out[SHIFT:STK, 0:QH], neg_max[:, u[2], :], ident[0:QH, 0:QH],
                                     start=True, stop=True).then_inc(made["shift"], 1)
                elif kind == "score":
                    p, j = u[2], u[3]
                    if p == 0 and j == 0:
                        reached(pe, stacked[t % 2], stack_count(b, t))
                        reached(pe, low_stacked, low_count(b, t))
                        reached(pe, shift_copied, count(b, "shift", t, 1))
                    reached(pe, exp_done, count(b, "score", t, p, j) - 2)
                    for k in range(2):
                        kt = 2 * p + k
                        last = nc.tensor.matmul(score_bank[j % 2][:, k * SQ:(k + 1) * SQ],
                                                kstack[t % 2][0:STK, j, kt * KW:kt * KW + P],
                                                qstack[t % 2][:, j, :], start=True, stop=True)
                    last.then_inc(made["score"], 1)
                elif kind == "pv":
                    p = u[2]
                    reached(pe, exp_done, count(b, "score", t, p, HG - 1))
                    if p == 0:
                        reached(pe, normalized, count(b, "sum", t - 2))
                        if t % 2 == 0:
                            reached(pe, v_copied, count(b, "v", 0, t // 2, KT - 1))
                    for k in range(2):
                        kt = 2 * p + k
                        for j in range(HG):
                            col = (t % 2) * P + j * DK
                            last = nc.tensor.matmul(pv_bank[t % 2][j * DK:(j + 1) * DK, 0:SQ],
                                                    values[:, t % NG // 2, kt, col:col + DK],
                                                    probs[p][:, j, k, :], start=(kt == 0), stop=(kt == KT - 1))
                    last.then_inc(made["pv"], 1)
                elif kind == "sum":
                    reached(pe, summed, 5 * (b * NG + t) + 5)
                    for j in range(HG):
                        last = nc.tensor.matmul(pv_bank[t % 2][j * DK:(j + 1) * DK, SQ:2 * SQ], ones[0:KW, :],
                                                prob_sum[:, j, :], start=True, stop=True)
                    last.then_inc(made["sum"], 1)

        phases(pe, body)

    @block.scalar
    def _(act):
        def body(b, units, proj_last, max_last):
            proj = mx = 0
            for u in units:
                kind, t = u[0], u[1]
                if kind in ("k", "q", "v", "xt", "out"):
                    src = proj_bank[proj % 2]
                    proj += 1
                if kind in ("max", "shift"):
                    mbank = max_bank[mx % 2]
                    mx += 1
                if kind == "score":
                    p, j = u[2], u[3]
                    act.wait_ge(made["score"], count(b, *u))
                    if j == 0:
                        reached(act, made["pv"], count(b, "pv", t - 1, p))
                        reached(act, summed, 5 * (b * NG + t - 1) + 2 * p + 1)
                    nc.scalar.activation(probs[p][:, j, :, :], score_bank[j % 2][0:KW, 0:2 * SQ].rearrange(
                        "p (k q) -> p k q", k=2), ACT.Exp, scale=float(DK) ** -0.5).then_inc(exp_done, 1)
                elif kind == "k":
                    lo, hi = KSPLIT[u[2]], KSPLIT[u[2] + 1]
                    act.wait_ge(made["k"], count(b, *u))
                    if u[2] == 0:
                        reached(act, stacked[t % 2], stack_count(b, t - 2))
                        reached(act, made["max"], count(b, "max", t - 2, 15))
                    nc.scalar.activation(k_part[t % 2][0][:, lo:hi], src[:, 0:hi - lo], ACT.Identity,
                                         bias=biases[:, 1, t % NG:t % NG + 1]).then_inc(hi_done["k"], 1)
                elif kind == "q":
                    act.wait_ge(made["q"], count(b, *u))
                    nc.scalar.activation(q_part[t % 2][0][:, :], src[:, 0:SQ], ACT.Identity,
                                         bias=biases[:, 0, t % NG:t % NG + 1]).then_inc(hi_done["q"], 1)
                elif kind == "v":
                    act.wait_ge(made["v"], count(b, *u))
                    if u[3] % 3 == 0:
                        reached(act, made["pv"], count(b, "pv", NG * (t - 1) + 2 * u[2] + 1, 2))
                    nc.scalar.activation(values[:, u[2], u[3], :], src[0:KW, 0:256], ACT.Copy).then_inc(v_copied, 1)
                elif kind == "xt":
                    act.wait_ge(made["xt"], count(b, *u))
                    reached(act, made["q"], count(b, "q", NG * t - 1))
                    nc.scalar.activation(xt_part[0][:, :, u[2] * QH:(u[2] + 1) * QH],
                                         src[:, 0:KC * QH].rearrange("p (c q) -> p c q", c=KC),
                                         ACT.Copy).then_inc(hi_done["xt"], 1)
                elif kind == "ctx":
                    reached(act, ctx_loaded, 16 * (b + t + 1))
                    if u[2] == 0:
                        reached(act, made["k"], count(b, "k", NG * t - 1, 1))
                        reached(act, made["v"], count(b, "v", t - 1, 1, KT - 1))
                    nc.scalar.activation(ctx_hi[:, u[2], 0:SK], ctx_raw[:, u[2], :], ACT.Copy)\
                        .then_inc(hi_done["ctx"], 1)
                elif kind == "shift":
                    act.wait_ge(made["shift"], count(b, *u))
                    row = mbank[SHIFT:STK, 0:QH].unsqueeze(1).to_broadcast([HG, HG, QH])
                    nc.scalar.activation(qstack[t % 2][SHIFT:STK, :, u[2] * QH:(u[2] + 1) * QH], row,
                                         ACT.Copy).then_inc(shift_copied, 1)
                elif kind == "sum":
                    reached(act, normalized, count(b, "sum", t))
                    if t % NG == 0:
                        reached(act, made["out"], count(b, "out", t // NG - 1, 1))
                    nc.scalar.activation(o_part[0][:, t % NG, :], heads[:, :], ACT.Identity,
                                         bias=biases[:, 2, t % NG:t % NG + 1]).then_inc(hi_done["sum"], 1)

        phases(act, body)

    @block.vector
    def _(dve):
        def body(b, units, proj_last, max_last):
            proj = mx = 0
            where = {}
            for u in units:
                kind, t = u[0], u[1]
                if kind in ("k", "q", "v", "xt", "out"):
                    where[u] = proj_bank[proj % 2]
                    proj += 1
                if kind in ("max", "shift"):
                    mbank = max_bank[mx % 2]
                    mx += 1
                if kind == "max":
                    half, j, kh = u[2] // 8, u[2] % 8 // 2, u[2] % 2
                    dve.wait_ge(made["max"], count(b, *u))
                    nc.vector.tensor_reduce(row_max[:, half, j, kh:kh + 1], mbank[0:QH, 0:KSPLIT[kh + 1] - KSPLIT[kh]],
                                            AX.X, ALU.max).then_inc(max_reduced, 1)
                    if u[2] % 8 == 7:
                        dve.wait_ge(max_reduced, count(b, *u))
                        reached(dve, made["shift"], count(b, "shift", t - 1, half))
                        nc.vector.tensor_reduce(neg_max[:, half, :], row_max[:, half, :, :], AX.X, ALU.max,
                                                negate=True).then_inc(max_negated, 1)
                elif kind == "k_lo":
                    k = ("k", t, u[2])
                    lo, hi = KSPLIT[u[2]], KSPLIT[u[2] + 1]
                    dve.wait_ge(hi_done["k"], count(b, *k))
                    if u[2] == 0:
                        reached(dve, stacked[t % 2], stack_count(b, t - 2))
                        reached(dve, low_stacked, low_count(b, t - 1))
                    nc.vector.scalar_tensor_tensor(k_part[t % 2][1][:, lo:hi], where[k][:, 0:hi - lo],
                                                   biases[:, 1, t % NG:t % NG + 1],
                                                   k_part[t % 2][0][:, lo:hi].bitcast(F32), ALU.add,
                                                   ALU.subtract).then_inc(lo_done["k"], 1)
                elif kind == "q_lo":
                    dve.wait_ge(hi_done["q"], count(b, "q", t))
                    nc.vector.scalar_tensor_tensor(q_part[t % 2][1][:, :], where[("q", t)][:, 0:SQ],
                                                   biases[:, 0, t % NG:t % NG + 1],
                                                   q_part[t % 2][0][:, :].bitcast(F32), ALU.add,
                                                   ALU.subtract).then_inc(lo_done["q"], 1)
                elif kind == "xt_lo":
                    k = ("xt", t, u[2])
                    dve.wait_ge(hi_done["xt"], count(b, *k))
                    part = slice(u[2] * QH, (u[2] + 1) * QH)
                    nc.vector.tensor_tensor(xt_part[1][:, :, part],
                                            where[k][:, 0:KC * QH].rearrange("p (c q) -> p c q", c=KC),
                                            xt_part[0][:, :, part].bitcast(F32), ALU.subtract)\
                        .then_inc(lo_done["xt"], 1)
                elif kind == "ctx":
                    dve.wait_ge(hi_done["ctx"], count(b, *u))
                    nc.vector.tensor_tensor(ctx_lo[:, u[2], 0:SK], ctx_raw[:, u[2], :],
                                            ctx_hi[:, u[2], 0:SK].bitcast(F32), ALU.subtract)\
                        .then_inc(lo_done["ctx"], 1)
                elif kind == "sum":
                    dve.wait_ge(made["sum"], count(b, "sum", t))
                    nc.vector.reciprocal(heads[:, :], pv_bank[t % 2][:, SQ:2 * SQ]).then_inc(inverted, 1)
                    dve.wait_ge(inverted, count(b, "sum", t))
                    nc.vector.tensor_tensor(heads[:, :], pv_bank[t % 2][:, 0:SQ], heads[:, :],
                                            ALU.mult).then_inc(normalized, 1)
                elif kind == "sum_lo":
                    dve.wait_ge(hi_done["sum"], count(b, "sum", t))
                    nc.vector.scalar_tensor_tensor(o_part[1][:, t % NG, :], heads[:, :],
                                                   biases[:, 2, t % NG:t % NG + 1],
                                                   o_part[0][:, t % NG, :].bitcast(F32), ALU.add,
                                                   ALU.subtract).then_inc(lo_done["sum"], 1)
                elif kind == "norm":
                    n = 2 * (b + t) + u[2]
                    reached(dve, x_loaded, 16 * (b + t + 1))
                    nc.vector.bn_stats(stats[:, u[2], :], xn[:, u[2], :]).then_inc(stats_done, 1)
                    dve.wait_ge(stats_done, n + 1)
                    nc.vector.memset(spacer[:, :], 0.0)
                    nc.vector.bn_aggr(mean_var[:, u[2], :], stats[:, u[2], :]).then_inc(var_done, 1)
                elif kind == "ffn_quant":
                    chain = 3 * b + t
                    if u[2] == 1:
                        dve.wait_ge(fw_loaded, 16 * chain + 16)
                    else:
                        dve.wait_ge(fw_steps, QSTEPS * chain + u[2] - 1)
                    part = fw_share[:, :]
                    quantize_step(nc, u[2], part, part, part, (fw_power, fw_share), fw_scales).then_inc(fw_steps, 1)
                elif kind == "norm2":
                    n = 2 * (b + t) + u[2]
                    dve.wait_ge(pow_steps, 2 * n + 2)
                    nc.vector.tensor_scalar(xn[:, u[2], :], xn[:, u[2], :], mean_var[:, u[2], 0:1],
                                            rstd[:, u[2]:u[2] + 1], ALU.subtract, ALU.mult).then_inc(xn_done, 1)
                elif kind == "out":
                    dve.wait_ge(made["out"], count(b, *u))
                    reached(dve, bias_added, 2 * (b + t) + u[2] + 1)
                    nc.vector.tensor_tensor(res[:, u[2], :], where[u][0:QH, :], res[:, u[2], :],
                                            ALU.add).then_inc(x1_done, 1)

        phases(dve, body)

    @block.gpsimd
    def _(pool):
        def body(b, units, proj_last, max_last):
            for u in units:
                kind, t = u[0], u[1]
                if kind == "pv":
                    p = u[2]
                    base = 5 * (b * NG + t)
                    pool.wait_ge(exp_done, count(b, "score", t, p, HG - 1))
                    if p == 0:
                        reached(pool, made["sum"], count(b, "sum", t - 1))
                        nc.gpsimd.tensor_tensor(prob_sum[:, :, :], probs[0][:, :, 0, :], probs[0][:, :, 1, :],
                                                ALU.add).then_inc(summed, 1)
                    else:
                        for k in range(2):
                            pool.wait_ge(summed, base + 2 * p - 1 + k)
                            nc.gpsimd.tensor_tensor(prob_sum[:, :, :], prob_sum[:, :, :], probs[p][:, :, k, :],
                                                    ALU.add).then_inc(summed, 1)
                elif kind == "norm":
                    n = 2 * (b + t) + u[2]
                    pool.wait_ge(var_done, n + 1)
                    nc.gpsimd.tensor_tensor(rstd[:, u[2]:u[2] + 1], mean_var[:, u[2], 1:2], ln_consts[0:QH, 1:2],
                                            ALU.add).then_inc(pow_steps, 1)
                    pool.wait_ge(pow_steps, 2 * n + 1)
                    nc.gpsimd.tensor_tensor(rstd[:, u[2]:u[2] + 1], rstd[:, u[2]:u[2] + 1], ln_consts[0:QH, 0:1],
                                            ALU.pow).then_inc(pow_steps, 1)
                elif kind == "load_res":
                    reached(pool, res_loaded, 16 * (b + t + 1))
                    for h in range(2):
                        nc.gpsimd.tensor_tensor(res[:, h, :], res[:, h, :], bo_rows[:, :], ALU.add)\
                            .then_inc(bias_added, 1)

        phases(pool, body)

    @block.sync
    def _(sp):
        def share_of(weights, m, b):
            return weights[m].rearrange("r c -> (r c)").rearrange("(p b k) -> b p k", p=P, k=share)[
                bass.ds(b, 1), :, :].rearrange("b p k -> (b p) k")

        heads_of = [slice(j * DK, (j + 1) * DK) for j in range(HG)]

        def rows(tensor, b, h=None):
            view = tensor.rearrange("b (h p) d -> b p h d", h=2)
            if h is None:
                return view[bass.ds(b, 1), :, :, :].rearrange("b p h d -> (b p) h d")
            return view[bass.ds(b, 1), :, h, :].rearrange("b p d -> (b p) d")

        def body(b, units, proj_last, max_last):
            for u in units:
                kind, t = u[0], u[1]
                if kind == "ffn_load":
                    reached(sp, fw_stored, 16 * (3 * b + t))
                    sp.dma_start(fw_share[:, :], share_of(ffn_raw, t, b)).then_inc(fw_loaded, 16)
                elif kind == "ffn_store":
                    chain = 3 * b + t
                    sp.wait_ge(fw_steps, QSTEPS * (chain + 1))
                    sp.dma_start(share_of(ffn_quant, t, b), fw_share[:, :]).then_inc(fw_stored, 16)
                elif kind == "load_ctx":
                    reached(sp, lo_done["ctx"], KC * (b + t))
                    sp.dma_start(ctx_raw[:, :, :], dram["ctx"][bass.ds(b + t, 1), :, :, :].rearrange(
                        "b p c s -> (b p) c s")).then_inc(ctx_loaded, 16)
                elif kind == "load_x":
                    reached(sp, made["xt"], 2 * (b + t))
                    sp.dma_start(xn[:, :, :], rows(dram["x"], b + t)).then_inc(x_loaded, 16)
                elif kind == "load_res":
                    reached(sp, x1_stored, 32 * (b + t))
                    sp.dma_start(res[:, :, :], rows(dram["x"], b + t)).then_inc(res_loaded, 16)
                elif kind == "out":
                    reached(sp, x1_done, count(b, *u))
                    sp.dma_start(rows(x1, b + t, u[2]), res[:, u[2], :]).then_inc(x1_stored, 16)
                elif kind == "stack_low":
                    par = t % 2
                    reached(sp, lo_done["q"], count(b, "q", t))
                    reached(sp, made["score"], count(b, "score", t - 2, 2, 3))
                    for j in range(HG):
                        sp.dma_start(kstack[par][2 * DK:3 * DK, j, 0:SK].bitcast(F32), k_low[heads_of[j], :].bitcast(F32))\
                            .then_inc(low_stacked, 16)
                elif kind == "stack":
                    par = t % 2
                    for j in range(HG):
                        for r in range(2):
                            sp.dma_start(kstack[par][heads_of[r], j, 0:SK].bitcast(F32),
                                         k_part[par][0][heads_of[j], :].bitcast(F32)).then_inc(stacked[par], 16)
                        for r, qp in enumerate((0, 1, 0)):
                            sp.dma_start(qstack[par][heads_of[r], j, :].bitcast(F32),
                                         q_part[par][qp][heads_of[j], :].bitcast(F32)).then_inc(stacked[par], 16)

        phases(sp, body)
        sp.wait_ge(x1_stored, 32 * batches)
        sp.wait_ge(fw_stored, 48 * batches)


def quantize_step(nc, n, x, a, out, work, scales):
    width = x.shape[1]
    nb = width // BLK
    amax, scale, inv = (s[:, 0:nb] for s in scales)
    power, t = (w[:, 0:width] for w in work)

    def blocks(ap):
        return ap.rearrange("p (n k) -> p n k", k=BLK)

    def spread(ap):
        return ap.unsqueeze(2).to_broadcast([P, nb, BLK])

    dve = nc.vector
    if n == 1:
        return dve.tensor_reduce(amax, blocks(x), AX.X, ALU.max, apply_absolute_value=True)
    if n == 2:
        return dve.tensor_scalar(scale, amax, 1.0 / 6.0, 1e-12, ALU.mult, ALU.max)
    if n == 3:
        return dve.reciprocal(inv, scale)
    if n == 4:
        return dve.tensor_tensor(blocks(a), blocks(x), spread(inv), ALU.mult)
    if n == 5:
        return dve.tensor_scalar(power.bitcast(U32), a.bitcast(U32), EXP_MASK, None, ALU.bitwise_and)
    if n == 6:
        return dve.tensor_scalar(power, power, 1.0, None, ALU.max)
    if n == 7:
        return dve.scalar_tensor_tensor(power.bitcast(U32), a.bitcast(U32), SIGN_MASK, power.bitcast(U32),
                                        ALU.bitwise_and, ALU.bitwise_or)
    if n == 8:
        return dve.scalar_tensor_tensor(t, power, TIE, a, ALU.mult, ALU.add)
    if n == 9:
        return dve.tensor_scalar(t.bitcast(U32), t.bitcast(U32), KEEP_MASK, None, ALU.bitwise_and)
    if n == 10:
        return dve.scalar_tensor_tensor(t, power, -2.0, t, ALU.mult, ALU.add)
    return dve.tensor_tensor(blocks(out), blocks(t), spread(scale), ALU.mult)


def quantize(nc, dve, steps, base, done, x, out, work, scales, width):
    a = work[0][:, 0:width]
    for n in range(1, QSTEPS):
        quantize_step(nc, n, x, a, out, work[1:], scales).then_inc(steps, 1)
        dve.wait_ge(steps, base + n)
    quantize_step(nc, QSTEPS, x, a, out, work[1:], scales).then_inc(done, 1)


def feed_forward_weights(nc, ctx, ffn_quant, ffn, ident):
    raw = [[ctx.enter_context(nc.sbuf_tensor(f"fw_raw{r}{n}", [P, D], F32)) for n in range(3)] for r in range(2)]
    banks = [ctx.enter_context(nc.psum_tensor(f"fw_bank{n}", [P, D], F32)) for n in range(3)]
    loaded = [[ctx.enter_context(nc.semaphore(f"fw_loaded{r}{n}")) for n in range(3)] for r in range(2)]
    turned = ctx.enter_context(nc.semaphore("fw_turned"))
    hi_done = ctx.enter_context(nc.semaphore("fw_hi_done"))
    lo_done = ctx.enter_context(nc.semaphore("fw_lo_done"))
    block = ctx.enter_context(nc.Block())

    def place(n, part, i):
        if n == 2:
            return ffn[2][part][:, bass.ds(i, 1), :].rearrange("p a (m n) -> p (a m) n", m=KC)
        return ffn[n][part][:, :, bass.ds(i * P, P)]

    def trips(engine, body):
        body(0, 0, 0)
        with engine.Fori(0, FC // 2) as i:
            body(2 * i + 1, 1, i)
            body(2 * i + 2, 0, i + 1)

    @block.sync
    def _(sp):
        views = [ffn_quant[0].rearrange("(i p) k -> i p k", p=P), ffn_quant[1].rearrange("(i p) k -> i p k", p=P),
                 ffn_quant[2].rearrange("(m p) (j k) -> j p m k", p=P, k=P)]

        def body(i, r, earlier):
            for n in range(3):
                reached(sp, turned, 3 * i - 5 + n)
                if n == 2:
                    sp.dma_start(raw[r][2][:, :].rearrange("p (m k) -> p m k", k=P),
                                 views[2][bass.ds(i, 1), :, :, :].rearrange("a p m k -> (a p) m k"))\
                        .then_inc(loaded[r][n], 16)
                else:
                    sp.dma_start(raw[r][n][:, :], views[n][bass.ds(i, 1), :, :].rearrange("a p k -> (a p) k"))\
                        .then_inc(loaded[r][n], 16)
        body(0, 0, 0)
        body(1, 1, 0)
        body(2, 0, 1)
        with sp.Fori(1, FC // 2) as i:
            body(2 * i + 1, 1, i)
            body(2 * i + 2, 0, i + 1)

    @block.tensor
    def _(pe):
        def body(i, r, earlier):
            for n in range(3):
                unit = 3 * i + n
                pe.wait_ge(loaded[r][n], 16 * earlier + 16)
                reached(pe, lo_done, unit - 2)
                for c in range(KC):
                    last = nc.tensor.transpose(banks[n][:, c * P:(c + 1) * P], raw[r][n][:, c * P:(c + 1) * P],
                                               ident[:, :])
                last.then_inc(turned, 1)
        trips(pe, body)

    @block.scalar
    def _(act):
        def body(i, r, earlier):
            for n in range(3):
                act.wait_ge(turned, 3 * i + n + 1)
                nc.scalar.activation(place(n, 0, i), banks[n][:, :].rearrange("p (c k) -> p c k", c=KC),
                                     ACT.Copy).then_inc(hi_done, 1)
        trips(act, body)

    @block.vector
    def _(dve):
        def body(i, r, earlier):
            for n in range(3):
                dve.wait_ge(hi_done, 3 * i + n + 1)
                nc.vector.tensor_tensor(place(n, 1, i), banks[n][:, :].rearrange("p (c k) -> p c k", c=KC),
                                        place(n, 0, i).bitcast(F32), ALU.subtract).then_inc(lo_done, 1)
        trips(dve, body)


def tile_units(t, first, last):
    units = []
    for c in range(3):
        q = 3 * t + c
        if c == 2 and not last:
            units.append(("turn_x", t + 1))
        units.append(("gate_up", q))
        if not (first and c == 0):
            units.append(("quant", q - 1))
        if not (first and c < 2):
            units += [("turn_h", q - 2), ("turn_h_lo", q - 2)]
        if not first:
            units.append(("down", q - 3))
        if c == 0 and not last:
            units.append(("load", t + 1))
        if c == 1 and not last:
            units.append(("norm", t + 1))
        if c == 2 and not last:
            units.append(("turn_x_lo", t + 1))
        if c == 2 and not first:
            units.append(("store", t - 1))
        if c == 0:
            units.append(("load_res", t))
    return units


def feed_forward(nc, ctx, x1, out, ffn, ident, ln_consts, tiles):
    def sb(name, shape, dt=F32):
        return ctx.enter_context(nc.sbuf_tensor(name, shape, dt))

    def bank(name):
        return ctx.enter_context(nc.psum_tensor(name, [P, 512], F32))

    def sem(name):
        return ctx.enter_context(nc.semaphore(name))

    xn = [sb(f"f_xn{i}", [P, D]) for i in range(2)]
    xq = sb("f_xq", [P, D])
    xqt = [[sb(f"f_xqt{i}{h}", [P, KC, P], F32R) for h in range(2)] for i in range(2)]
    act_gate = [sb(f"f_act_gate{i}", [P, 512]) for i in range(2)]
    hidden = sb("f_hidden", [P, 512])
    work = [sb(f"f_work{i}", [P, 512]) for i in range(3)]
    scales = [sb(f"f_scale{i}", [P, 512 // BLK]) for i in range(3)]
    hq = [sb(f"f_hq{c}", [P, 512]) for c in range(3)]
    hqt = [sb(f"f_hqt{h}", [P, FC, P], F32R) for h in range(2)]
    res = [sb(f"f_res{i}", [P, D]) for i in range(2)]
    stats = sb("f_stats", [P, 6])
    mean_var = sb("f_mean_var", [P, 2])
    rstd = sb("f_rstd", [P, 1])
    spacer = sb("f_spacer", [P, 1])

    gate_bank = [bank(f"gate_bank{i}") for i in range(2)]
    up_bank = [bank(f"up_bank{i}") for i in range(2)]
    turn_bank = [bank(f"turn_bank{i}") for i in range(2)]
    down_bank = [bank(f"down_bank{i}") for i in range(2)]

    x_loaded = [sem(f"f_x_loaded{i}") for i in range(2)]
    res_loaded = [sem(f"f_res_loaded{i}") for i in range(2)]
    stored = [sem(f"f_stored{i}") for i in range(2)]
    ln_steps = sem("f_ln_steps")
    pow_steps = sem("f_pow_steps")
    x_normed = sem("f_x_normed")
    x_steps = sem("f_x_quant_steps")
    x_quantized = sem("f_x_quantized")
    x_turned = sem("f_x_turned")
    x_hi = sem("f_x_hi")
    x_lo = sem("f_x_lo")
    gated = sem("f_gate_up_made")
    silu_done = sem("f_silu_done")
    hidden_done = sem("f_hidden_done")
    h_steps = sem("f_h_quant_steps")
    h_quantized = sem("f_h_quantized")
    h_turned = sem("f_h_turned")
    h_hi = sem("f_h_hi")
    h_lo = sem("f_h_lo")
    down_made = sem("f_down_made")
    down_part = sem("f_down_part")
    y_done = sem("f_y_done")

    def phases(engine, body):
        body(0, start)
        body(0, tile_units(0, True, False) + tile_units(1, False, False))
        with engine.Fori(1, tiles // 2 - 1) as i:
            body(i, tile_units(0, False, False) + tile_units(1, False, False))
        body(tiles // 2 - 1, tile_units(0, False, False) + tile_units(1, False, True))
        body(tiles // 2 - 1, finish)

    start = [("load", 0), ("norm", 0), ("turn_x", 0), ("turn_x_lo", 0)]
    finish = [("quant", 5), ("turn_h", 4), ("turn_h_lo", 4), ("down", 3), ("turn_h", 5), ("turn_h_lo", 5),
              ("down", 4), ("down", 5), ("store", 1)]

    block = ctx.enter_context(nc.Block())

    @block.sync
    def _(sp):
        xs = x1.rearrange("b s d -> (b s) d").rearrange("(n p) d -> n p d", p=P)
        ys = out.rearrange("b s d -> (b s) d").rearrange("(n p) d -> n p d", p=P)

        def body(i, units):
            for kind, n in units:
                tile = 2 * i + n
                if kind == "load":
                    reached(sp, x_quantized, tile - 1)
                    sp.dma_start(xn[n % 2][:, :], xs[bass.ds(tile, 1), :, :].rearrange("a p d -> (a p) d"))\
                        .then_inc(x_loaded[n % 2], 16)
                elif kind == "load_res":
                    reached(sp, stored[n % 2], 16 * (i + n // 2))
                    sp.dma_start(res[n % 2][:, :], xs[bass.ds(tile, 1), :, :].rearrange("a p d -> (a p) d"))\
                        .then_inc(res_loaded[n % 2], 16)
                elif kind == "store":
                    reached(sp, y_done, tile + 1)
                    sp.dma_start(ys[bass.ds(tile, 1), :, :].rearrange("a p d -> (a p) d"), res[n % 2][:, :])\
                        .then_inc(stored[n % 2], 16)
        phases(sp, body)
        for par in range(2):
            sp.wait_ge(stored[par], 16 * (tiles // 2))

    @block.tensor
    def _(pe):
        def body(i, units):
            for kind, n in units:
                if kind == "turn_x":
                    tile = 2 * i + n
                    reached(pe, x_quantized, tile + 1)
                    reached(pe, x_lo, tile)
                    for c in range(KC):
                        last = nc.tensor.transpose(turn_bank[0][:, c * P:(c + 1) * P], xq[:, c * P:(c + 1) * P],
                                                   ident[:, :])
                    last.then_inc(x_turned, 1)
                elif kind == "gate_up":
                    q = 6 * i + n
                    t, c = n // 3, n % 3
                    reached(pe, x_lo, 2 * i + t + 1)
                    reached(pe, hidden_done, q - 1)
                    lo, hi = CH[c], CH[c + 1]
                    for w, banks in ((0, gate_bank), (1, up_bank)):
                        k = 0
                        for kc in range(KC):
                            for xs_, ws in PASSES:
                                last = nc.tensor.matmul(banks[n % 2][:, 0:hi - lo], xqt[t % 2][xs_][:, kc, :],
                                                        ffn[w][ws][:, kc, lo:hi], start=(k == 0), stop=(k == 11))
                                k += 1
                    last.then_inc(gated, 1)
                elif kind == "turn_h":
                    q = 6 * i + n
                    c = n % 3
                    reached(pe, h_quantized, q + 1)
                    reached(pe, h_lo, q)
                    for m in range((CH[c + 1] - CH[c]) // P):
                        last = nc.tensor.transpose(turn_bank[1][:, m * P:(m + 1) * P], hq[c][:, m * P:(m + 1) * P],
                                                   ident[:, :])
                    last.then_inc(h_turned, 1)
                elif kind == "down":
                    q = 6 * i + n
                    t, c = n // 3, n % 3
                    reached(pe, h_lo, q + 1)
                    if c == 0:
                        reached(pe, y_done, 2 * i + t - 1)
                    lo, hi = CH[c] // P, CH[c + 1] // P
                    for m in range(lo, hi):
                        for k, (hs, ws) in enumerate(PASSES):
                            last = nc.tensor.matmul(down_bank[t % 2][:, :], hqt[hs][:, m, :], ffn[2][ws][:, m, :],
                                                    start=(m == 0 and k == 0), stop=(m == FC - 1 and k == 2))
                    last.then_inc(down_part, 1)
        phases(pe, body)

    @block.scalar
    def _(act):
        def body(i, units):
            for kind, n in units:
                if kind == "turn_x":
                    tile = 2 * i + n
                    act.wait_ge(x_turned, tile + 1)
                    nc.scalar.activation(xqt[n % 2][0][:, :, :], turn_bank[0][:, :].rearrange(
                        "p (c k) -> p c k", c=KC), ACT.Copy).then_inc(x_hi, 1)
                elif kind == "gate_up":
                    q = 6 * i + n
                    w = CH[n % 3 + 1] - CH[n % 3]
                    act.wait_ge(gated, q + 1)
                    reached(act, hidden_done, q - 1)
                    nc.scalar.activation(act_gate[n % 2][:, 0:w], gate_bank[n % 2][:, 0:w],
                                         ACT.Silu).then_inc(silu_done, 1)
                elif kind == "turn_h":
                    q = 6 * i + n
                    lo, hi = CH[n % 3] // P, CH[n % 3 + 1] // P
                    act.wait_ge(h_turned, q + 1)
                    reached(act, down_part, q - 2)
                    nc.scalar.activation(hqt[0][:, lo:hi, :], turn_bank[1][:, 0:(hi - lo) * P].rearrange(
                        "p (m k) -> p m k", k=P), ACT.Copy).then_inc(h_hi, 1)
        phases(act, body)

    @block.gpsimd
    def _(pool):
        def body(i, units):
            for kind, n in units:
                if kind == "norm":
                    tile = 2 * i + n
                    pool.wait_ge(ln_steps, 2 * tile + 2)
                    nc.gpsimd.tensor_tensor(rstd[:, :], mean_var[:, 1:2], ln_consts[:, 1:2],
                                            ALU.add).then_inc(pow_steps, 1)
                    pool.wait_ge(pow_steps, 2 * tile + 1)
                    nc.gpsimd.tensor_tensor(rstd[:, :], rstd[:, :], ln_consts[:, 0:1],
                                            ALU.pow).then_inc(pow_steps, 1)
        phases(pool, body)

    @block.vector
    def _(dve):
        def body(i, units):
            for kind, n in units:
                if kind == "norm":
                    tile = 2 * i + n
                    dve.wait_ge(x_loaded[n % 2], 16 * (i + n // 2) + 16)
                    nc.vector.bn_stats(stats[:, :], xn[n % 2][:, :]).then_inc(ln_steps, 1)
                    dve.wait_ge(ln_steps, 2 * tile + 1)
                    nc.vector.memset(spacer[:, :], 0.0)
                    nc.vector.bn_aggr(mean_var[:, :], stats[:, :]).then_inc(ln_steps, 1)
                    dve.wait_ge(pow_steps, 2 * tile + 2)
                    nc.vector.tensor_scalar(xn[n % 2][:, :], xn[n % 2][:, :], mean_var[:, 0:1], rstd[:, :],
                                            ALU.subtract, ALU.mult).then_inc(x_normed, 1)
                    dve.wait_ge(x_normed, tile + 1)
                    reached(dve, x_turned, tile)
                    quantize(nc, dve, x_steps, (QSTEPS - 1) * tile, x_quantized, xn[n % 2][:, :], xq[:, :], work,
                             scales, D)
                elif kind == "turn_x_lo":
                    tile = 2 * i + n
                    dve.wait_ge(x_hi, tile + 1)
                    nc.vector.tensor_tensor(xqt[n % 2][1][:, :, :], turn_bank[0][:, :].rearrange(
                        "p (c k) -> p c k", c=KC), xqt[n % 2][0][:, :, :].bitcast(F32), ALU.subtract)\
                        .then_inc(x_lo, 1)
                elif kind == "quant":
                    q = 6 * i + n
                    c = n % 3
                    w = CH[c + 1] - CH[c]
                    reached(dve, silu_done, q + 1)
                    nc.vector.tensor_tensor(hidden[:, 0:w], act_gate[n % 2][:, 0:w], up_bank[n % 2][:, 0:w],
                                            ALU.mult).then_inc(hidden_done, 1)
                    dve.wait_ge(hidden_done, q + 1)
                    reached(dve, h_turned, q - 2)
                    quantize(nc, dve, h_steps, (QSTEPS - 1) * q, h_quantized, hidden[:, 0:w], hq[c][:, 0:w], work,
                             scales, w)
                elif kind == "turn_h_lo":
                    q = 6 * i + n
                    lo, hi = CH[n % 3] // P, CH[n % 3 + 1] // P
                    reached(dve, h_hi, q + 1)
                    nc.vector.tensor_tensor(hqt[1][:, lo:hi, :], turn_bank[1][:, 0:(hi - lo) * P].rearrange(
                        "p (m k) -> p m k", k=P), hqt[0][:, lo:hi, :].bitcast(F32), ALU.subtract)\
                        .then_inc(h_lo, 1)
                elif kind == "store":
                    tile = 2 * i + n
                    reached(dve, down_part, 3 * tile + 3)
                    reached(dve, res_loaded[n % 2], 16 * (i + n // 2) + 16)
                    nc.vector.tensor_tensor(res[n % 2][:, :], down_bank[n % 2][:, :], res[n % 2][:, :],
                                            ALU.add).then_inc(y_done, 1)
        phases(dve, body)


def cross_attention_ffn(nc, dram, out):
    batches = dram["x"].shape[0]
    x1 = nc.dram_tensor("x1_scratch", (batches, SQ, D), F32, kind="Internal").ap()
    ffn_raw = [dram[n] for n in ("gate", "up", "down")]
    ffn_quant = [nc.dram_tensor(f"ffn_quant{n}", w.shape, F32, kind="Internal").ap() for n, w in enumerate(ffn_raw)]
    with ExitStack() as whole:
        def keep(name, shape, dt=F32, stack=whole):
            return stack.enter_context(nc.sbuf_tensor(name, shape, dt))

        ident = keep("ident", [P, P])
        ln_consts = keep("ln_consts", [P, 2])
        with ExitStack() as first_half:
            w_hi_lo = [[keep(f"w{n}_{h}", [P, KC, D], F32R, first_half) for h in ("hi", "lo")]
                       for n in ("q", "k", "v", "o")]
            consts = ([keep(f"kstack{i}", [STK, HG, SKP], F32R, first_half) for i in range(2)],
                      keep("ctx_hi", [P, KC, SKP], F32R, first_half),
                      keep("ctx_lo", [P, KC, SKP], F32R, first_half), ident,
                      keep("ones", [P, DK], F32, first_half), ln_consts,
                      keep("biases", [P, 3, KC], F32, first_half), keep("bo_rows", [QH, D], F32, first_half))
            with ExitStack() as ctx:
                attention_weights(nc, ctx, dram, w_hi_lo, consts)
            with ExitStack() as ctx:
                attention(nc, ctx, dram, w_hi_lo, consts, x1, ffn_raw, ffn_quant, batches)
        ffn = [[keep(f"ffn_{n}_{h}", [P, KC, F] if n != "down" else [P, FC, D], F32R) for h in ("hi", "lo")]
               for n in ("gate", "up", "down")]
        with ExitStack() as ctx:
            feed_forward_weights(nc, ctx, ffn_quant, ffn, ident)
        with ExitStack() as ctx:
            feed_forward(nc, ctx, x1, out, ffn, ident, ln_consts, batches * SQ // P)


def kernel(x, ctx_1024, L0_xattn_Wq, L0_xattn_bq, L0_xattn_Wk, L0_xattn_bk, L0_xattn_Wv, L0_xattn_bv,
           L0_xattn_Wo, L0_xattn_bo, L0_ffn_w_gate, L0_ffn_w_up, L0_ffn_w_down):
    import numpy as np
    import concourse.bacc as bacc
    from concourse.bass_utils import run_bass_kernel_spmd

    nc = bacc.Bacc("TRN2", target_bir_lowering=False, num_devices=1)
    batches = x.shape[0]

    def turned(w):
        return np.ascontiguousarray(np.asarray(w).T.reshape(KC, P, D).transpose(1, 0, 2))

    def columns(b):
        return np.ascontiguousarray(np.asarray(b).reshape(KC, P).T)

    arrays = {
        "x": np.ascontiguousarray(x),
        "ctx": np.ascontiguousarray(np.asarray(ctx_1024).reshape(batches, SK, KC, P).transpose(0, 3, 2, 1)),
        "wq": turned(L0_xattn_Wq), "wk": turned(L0_xattn_Wk), "wv": turned(L0_xattn_Wv), "wo": turned(L0_xattn_Wo),
        "bq": columns(L0_xattn_bq), "bk": columns(L0_xattn_bk), "bv": columns(L0_xattn_bv),
        "bo": np.ascontiguousarray(L0_xattn_bo),
        "gate": np.ascontiguousarray(L0_ffn_w_gate), "up": np.ascontiguousarray(L0_ffn_w_up),
        "down": np.ascontiguousarray(L0_ffn_w_down),
    }
    dram = {n: nc.dram_tensor(f"in_{n}", a.shape, mybir.dt.from_np(a.dtype), kind="ExternalInput").ap()
            for n, a in arrays.items()}
    out = nc.dram_tensor("out_0", x.shape, F32, kind="ExternalOutput").ap()
    cross_attention_ffn(nc, dram, out)
    result = run_bass_kernel_spmd(nc, [{f"in_{n}": a for n, a in arrays.items()}], core_ids=[0])
    return result.results[0]["out_0"]
```

```python
import concourse.bass as bass
from concourse import mybir
from contextlib import ExitStack

F32 = mybir.dt.float32
F32R = mybir.dt.float32r
U32 = mybir.dt.uint32
ALU = mybir.AluOpType
ACT = mybir.ActivationFunctionType
AX = mybir.AxisListType

P = 128
D = 512
KC = D // P
DK = 32
HG = P // DK
NG = D // P
SQ = 224
QH = SQ // 2
SK = 750
KT = 6
KW = SK // KT
SKP = (KT - 1) * KW + P + 1
KSPLIT = (0, 376, SK)
SHIFT = 3 * DK
STK = SHIFT + HG
F = 1408
FC = F // P
CH = (0, 512, 1024, F)
BLK = 16
WU = 2 * FC + FC
EPS = 1e-5
PASSES = ((0, 0), (0, 1), (1, 0))
EXP_MASK = 0x7F800000
SIGN_MASK = 0x80000000
KEEP_MASK = 0xFFE00000
TIE = 2.25 - 2.0 ** -22
QSTEPS = 11


def reached(engine, sem, count):
    if not isinstance(count, int) or count > 0:
        engine.wait_ge(sem, count)


def attention_weights(nc, ctx, dram, w_hi_lo, consts):
    raw = [ctx.enter_context(nc.sbuf_tensor(f"w_raw{i}", [P, KC, D], F32)) for i in range(2)]
    loaded = [ctx.enter_context(nc.semaphore(f"w_loaded{i}")) for i in range(2)]
    small_loaded = ctx.enter_context(nc.semaphore("small_loaded"))
    hi_done = ctx.enter_context(nc.semaphore("w_hi_done"))
    lo_done = ctx.enter_context(nc.semaphore("w_lo_done"))
    zeroed = ctx.enter_context(nc.semaphore("consts_zeroed"))
    made = ctx.enter_context(nc.semaphore("consts_made"))
    pick = ctx.enter_context(nc.sbuf_tensor("pick", [STK, HG, SKP], F32))
    kstack, ctx_hi, ctx_lo, ident, ones, ln_consts, biases, bo_rows = consts
    block = ctx.enter_context(nc.Block())

    @block.sync
    def _(sp):
        for n, src in enumerate((dram["bq"], dram["bk"], dram["bv"])):
            sp.dma_start(biases[:, n, :], src).then_inc(small_loaded, 16)
        sp.dma_start(bo_rows[:, :], dram["bo"].partition_broadcast(QH)).then_inc(small_loaded, 16)
        for n, name in enumerate(("wq", "wk", "wv", "wo")):
            if n >= 2:
                sp.wait_ge(lo_done, n - 1)
            sp.dma_start(raw[n % 2][:, :, :], dram[name]).then_inc(loaded[n % 2], 16)
        sp.wait_ge(small_loaded, 64)

    @block.scalar
    def _(act):
        for n in range(4):
            act.wait_ge(loaded[n % 2], 16 * (n // 2 + 1))
            nc.scalar.activation(w_hi_lo[n][0][:, :, :], raw[n % 2][:, :, :], ACT.Copy).then_inc(hi_done, 1)
        act.wait_ge(made, 2)
        for par in range(2):
            nc.scalar.activation(kstack[par][SHIFT:STK, :, :], pick[SHIFT:STK, :, :], ACT.Copy)

    @block.vector
    def _(dve):
        nc.vector.memset(ones[:, :], 1.0)
        nc.vector.memset(ln_consts[:, 0:1], -0.5)
        nc.vector.memset(ln_consts[:, 1:2], EPS)
        for n in range(4):
            dve.wait_ge(hi_done, n + 1)
            nc.vector.tensor_tensor(w_hi_lo[n][1][:, :, :], raw[n % 2][:, :, :],
                                    w_hi_lo[n][0][:, :, :].bitcast(F32), ALU.subtract).then_inc(lo_done, 1)

    @block.gpsimd
    def _(pool):
        nc.gpsimd.memset(ident[:, :], 0.0).then_inc(zeroed, 1)
        for par in range(2):
            nc.gpsimd.memset(kstack[par][:, :, :].bitcast(F32), 0.0).then_inc(zeroed, 1)
        nc.gpsimd.memset(ctx_hi[:, :, SK:SKP].bitcast(F32), 0.0)
        nc.gpsimd.memset(ctx_lo[:, :, SK:SKP].bitcast(F32), 0.0).then_inc(zeroed, 1)
        pool.wait_ge(zeroed, 4)
        nc.gpsimd.memset(pick[SHIFT:STK, :, :], 0.0).then_inc(zeroed, 1)
        pool.wait_ge(zeroed, 5)
        nc.gpsimd.affine_select(out=ident[:, :], in_=ident[:, :], compare_op=ALU.not_equal, fill=1.0,
                                base=0, pattern=[[-1, P]], channel_multiplier=1).then_inc(made, 1)
        pool.wait_ge(made, 1)
        nc.gpsimd.affine_select(out=pick[SHIFT:STK, :, :], in_=pick[SHIFT:STK, :, :], compare_op=ALU.not_equal,
                                fill=1.0, base=0, pattern=[[-1, HG], [0, SKP]], channel_multiplier=1)\
            .then_inc(made, 1)


FFN_SLOTS = (0, 1, 3)
FFN_STEPS = ((), (), (), (1,), (2, 3), (4,), (5,), (6,), (7,), (8,), (9,), (10, 11))
MAX_STEPS = (2, 1, 2, 1, 2, 1, 2, 1, 2, 1, 1, 0)


def slot_units(g, first, last):
    units = []
    maxima = 0
    for i in range(12):
        p, j = i // 4, i % 4
        units.append(("score", g, p, j))
        if i == 0:
            if not (last and g == 3):
                units.append(("stack_low", g + 1))
            if g in FFN_SLOTS:
                units.append(("ffn_load", FFN_SLOTS.index(g)))
            if not (last and g == 3):
                units.append(("stack", g + 1))
        if not (first and g == 0):
            if i == 1:
                units.append(("pv", g - 1, 2))
            if i == 8:
                units += [("sum", g - 1)]
            if i == 10:
                units += [("sum_lo", g - 1)]
        if i in (5, 9):
            units.append(("pv", g, i // 4 - 1))
        if not (last and g == 3):
            for _ in range(MAX_STEPS[i]):
                units.append(("max", g + 1, maxima))
                maxima += 1
            if i in (7, 11):
                units.append(("shift", g + 1, i // 8))
        if g in FFN_SLOTS:
            m = FFN_SLOTS.index(g)
            units += [("ffn_quant", m, n) for n in FFN_STEPS[i]]
            if i == 11:
                units.append(("ffn_store", m))
        if g == 1 and not first:
            if i in (2, 3):
                units.append(("out", -1, i - 2))
        if g == 2 and not last:
            if i < 4:
                units.append(("ctx", 1, i))
            if i in (2, 3):
                units.append(("xt", 1, i - 2))
            if i in (3, 4):
                units.append(("xt_lo", 1, i - 3))
        if g == 1 and not last:
            if i in (5, 6):
                units.append(("norm", 1, i - 5))
            if i in (8, 9):
                units.append(("norm2", 1, i - 8))
        if g == 0 and i == 2 and not last:
            units += [("load_ctx", 1), ("load_x", 1)]
        if g == 3 and i == 6:
            units.append(("load_res", 0))
        if g < 2 or not last:
            units += {4: [("k", g + 2, 0)], 5: [("k", g + 2, 1), ("k_lo", g + 2, 0)],
                      6: [("q", g + 2), ("k_lo", g + 2, 1)], 7: [("q_lo", g + 2)]}.get(i, [])
            if i in (8, 10, 11):
                half = 1 if g < 2 else 0
                units.append(("v", 0 if g < 2 else 1, half, 3 * (g % 2) + {8: 0, 10: 1, 11: 2}[i]))
    return units


def batch_units(first, last):
    return [u for g in range(NG) for u in slot_units(g, first, last)]


def start_units():
    units = [("load_ctx", 0), ("load_x", 0)]
    units += [("norm", 0, 0), ("norm", 0, 1), ("norm2", 0, 0), ("norm2", 0, 1)]
    units += [("ctx", 0, c) for c in range(KC)]
    units += [("xt", 0, 0), ("xt", 0, 1), ("xt_lo", 0, 0), ("xt_lo", 0, 1)]
    for t in range(2):
        units += [("k", t, 0), ("k", t, 1), ("k_lo", t, 0), ("q", t), ("k_lo", t, 1), ("q_lo", t)]
        if t == 0:
            units += [("stack_low", 0), ("stack", 0)]
    units += [("v", 0, 0, n) for n in range(KT)]
    return units + [(u[0], 0, u[2]) for u in slot_units(NG - 1, True, False) if u[0] in ("max", "shift")]


END_UNITS = [("pv", 3, 2), ("sum", 3), ("sum_lo", 3), ("out", 0, 0), ("out", 0, 1)]


def attention(nc, ctx, dram, w_hi_lo, consts, x1, ffn_raw, ffn_quant, batches):
    def sb(name, shape, dt=F32):
        return ctx.enter_context(nc.sbuf_tensor(name, shape, dt))

    def bank(name):
        return ctx.enter_context(nc.psum_tensor(name, [P, 512], F32))

    def sem(name):
        return ctx.enter_context(nc.semaphore(name))

    kstack, ctx_hi, ctx_lo, ident, ones, ln_consts, biases, bo_rows = consts
    ctx_raw = sb("ctx_raw", [P, KC, SK])
    ctx_part = (ctx_hi, ctx_lo)
    qstack = [sb(f"qstack{i}", [STK, HG, SQ], F32R) for i in range(2)]
    k_low = sb("k_low", [P, SK], F32R)
    k_part = [[sb(f"k_high{i}", [P, SK], F32R), k_low] for i in range(2)]
    q_part = [[sb(f"q_part{i}{h}", [P, SQ], F32R) for h in range(2)] for i in range(2)]
    values = sb("values", [KW, 2, KT, 256])
    probs = [sb(f"probs{p}", [KW, HG, 2, SQ]) for p in range(3)]
    prob_sum = sb("prob_sum", [KW, HG, SQ])
    heads = sb("heads", [P, SQ])
    o_part = [sb(f"o_part{h}", [P, NG, SQ], F32R) for h in range(2)]
    xn = sb("xn", [QH, 2, D])
    xt_part = [sb(f"xt_part{h}", [P, KC, SQ], F32R) for h in range(2)]
    res = sb("res", [QH, 2, D])
    share = F * D // (P * batches)
    fw_share, fw_power = sb("fw_share", [P, share]), sb("fw_power", [P, share])
    fw_scales = [sb(f"fw_{n}", [P, share // BLK]) for n in ("amax", "scale", "inv_scale")]
    stats = sb("stats", [QH, 2, 6])
    mean_var = sb("mean_var", [QH, 2, 2])
    rstd = sb("rstd", [QH, 2])
    spacer = sb("spacer", [P, 1])
    row_max = sb("row_max", [QH, 2, HG, 2])
    neg_max = sb("neg_max", [QH, 2, HG])

    score_bank = [bank(f"score_bank{i}") for i in range(2)]
    max_bank = [bank(f"max_bank{i}") for i in range(2)]
    proj_bank = [bank(f"proj_bank{i}") for i in range(2)]
    pv_bank = [bank(f"pv_bank{i}") for i in range(2)]

    names = ("score", "max", "shift", "k", "q", "v", "xt", "out", "pv", "sum")
    made = {n: sem(f"{n}_made") for n in names}
    exp_done = sem("exp_done")
    hi_done = {n: sem(f"{n}_hi_done") for n in ("k", "q", "xt", "ctx", "sum")}
    lo_done = {n: sem(f"{n}_lo_done") for n in ("k", "q", "xt", "ctx", "sum")}
    v_copied = sem("v_copied")
    shift_copied = sem("shift_copied")
    max_reduced = sem("max_reduced")
    max_negated = sem("max_negated")
    inverted = sem("sum_inverted")
    normalized = sem("heads_normalized")
    summed = sem("probs_summed")
    stats_done = sem("ln_stats")
    var_done = sem("ln_var")
    pow_steps = sem("ln_pow_steps")
    xn_done = sem("xn_done")
    bias_added = sem("res_bias_added")
    x1_done = sem("x1_done")
    ctx_loaded = sem("ctx_loaded")
    x_loaded = sem("x_loaded")
    res_loaded = sem("res_loaded")
    x1_stored = sem("x1_stored")
    stacked = [sem(f"stacked{i}") for i in range(2)]
    low_stacked = sem("low_stacked")
    fw_loaded = sem("fw_share_loaded")
    fw_steps = sem("fw_quant_steps")
    fw_stored = sem("fw_share_stored")
    STACK_DMAS = 5 * HG

    def index_of(unit, b):
        kind = unit[0]
        if kind == "v":
            return ((b + unit[1]) * 2 + unit[2]) * KT + unit[3]
        per = {"score": 12, "max": 16, "shift": 2, "k": 2, "q": 1, "pv": 3, "sum": 1}
        if kind in per:
            place = unit[2] * 4 + unit[3] if kind == "score" else unit[2] if len(unit) > 2 else 0
            return (b * NG + unit[1]) * per[kind] + place
        return (b + unit[1]) * {"xt": 2, "out": 2, "ctx": KC}[kind] + unit[2]

    def count(b, *unit):
        return index_of(unit, b) + 1

    def stack_count(b, t):
        return (b * (NG // 2) + t // 2 + 1) * 16 * STACK_DMAS

    def low_count(b, t):
        return (b * NG + t + 1) * 16 * HG

    def freed(engine, unit, b):
        kind = unit[0]
        done = {"k": lo_done["k"], "q": lo_done["q"], "xt": lo_done["xt"], "v": v_copied, "out": x1_done,
                "max": max_reduced, "shift": shift_copied}[kind]
        reached(engine, done, count(b, *unit))

    def phases(engine, body):
        body(0, start_units(), [None, None], [None, None])
        v_end = [("v", 0, 0, KT - 2), ("v", 0, 0, KT - 1)]
        m_end = [("max", 0, 15), ("shift", 0, 1)]
        body(0, batch_units(True, False), list(v_end), list(m_end))
        with engine.Fori(1, batches - 1) as b:
            body(b, batch_units(False, False), list(v_end), list(m_end))
        v_last = [("v", 0, 1, KT - 2), ("v", 0, 1, KT - 1)]
        body(batches - 1, batch_units(False, True), list(v_end), list(m_end))
        body(batches - 1, END_UNITS, v_last, [None, None])

    block = ctx.enter_context(nc.Block())

    @block.tensor
    def _(pe):
        def body(b, units, proj_last, max_last):
            proj = mx = 0
            for u in units:
                kind, t = u[0], u[1]
                if kind in ("k", "q", "v", "xt", "out"):
                    out = proj_bank[proj % 2]
                    if proj_last[proj % 2] is not None:
                        freed(pe, proj_last[proj % 2], b)
                    proj_last[proj % 2] = u
                    proj += 1
                if kind in ("max", "shift"):
                    out = max_bank[mx % 2]
                    if max_last[mx % 2] is not None:
                        freed(pe, max_last[mx % 2], b)
                    max_last[mx % 2] = u
                    mx += 1
                if kind == "k":
                    lo, hi = KSPLIT[u[2]], KSPLIT[u[2] + 1]
                    g = t % NG
                    if g == 0 and u[2] == 0:
                        reached(pe, lo_done["ctx"], count(b, "ctx", t // NG, KC - 1))
                    n = 0
                    for c in range(KC):
                        for ws, cs in PASSES:
                            last = nc.tensor.matmul(out[:, 0:hi - lo], w_hi_lo[1][ws][:, c, g * P:(g + 1) * P],
                                                    ctx_part[cs][:, c, lo:hi], start=(n == 0), stop=(n == 11))
                            n += 1
                    last.then_inc(made["k"], 1)
                elif kind == "q":
                    g = t % NG
                    if g == 0:
                        reached(pe, lo_done["xt"], count(b, "xt", t // NG, 1))
                    n = 0
                    for c in range(KC):
                        for ws, cs in PASSES:
                            last = nc.tensor.matmul(out[:, 0:SQ], w_hi_lo[0][ws][:, c, g * P:(g + 1) * P],
                                                    xt_part[cs][:, c, :], start=(n == 0), stop=(n == 11))
                            n += 1
                    last.then_inc(made["q"], 1)
                elif kind == "v":
                    half, kt = u[2], u[3]
                    n = 0
                    for c in range(KC):
                        for cs, ws in PASSES:
                            last = nc.tensor.matmul(out[:, 0:256], ctx_part[cs][:, c, kt * KW:kt * KW + P],
                                                    w_hi_lo[2][ws][:, c, half * 256:(half + 1) * 256],
                                                    start=(n == 0), stop=(n == 11))
                            n += 1
                    last.then_inc(made["v"], 1)
                elif kind == "xt":
                    reached(pe, xn_done, 2 * (b + t) + u[2] + 1)
                    for c in range(KC):
                        last = nc.tensor.transpose(out[:, c * QH:(c + 1) * QH], xn[:, u[2], c * P:(c + 1) * P],
                                                   ident[0:QH, 0:QH])
                    last.then_inc(made["xt"], 1)
                elif kind == "out":
                    reached(pe, lo_done["sum"], count(b, "sum", NG * t + 3))
                    n = 0
                    for g in range(NG):
                        for os_, ws in PASSES:
                            last = nc.tensor.matmul(out[0:QH, :], o_part[os_][:, g, u[2] * QH:(u[2] + 1) * QH],
                                                    w_hi_lo[3][ws][:, g, :], start=(n == 0), stop=(n == 11))
                            n += 1
                    last.then_inc(made["out"], 1)
                elif kind == "max":
                    half, j, kh = u[2] // 8, u[2] % 8 // 2, u[2] % 2
                    if u[2] == 0:
                        reached(pe, hi_done["k"], count(b, "k", t, 1))
                        reached(pe, hi_done["q"], count(b, "q", t))
                    lo, hi = KSPLIT[kh], KSPLIT[kh + 1]
                    rows = slice(j * DK, (j + 1) * DK)
                    nc.tensor.matmul(out[0:QH, 0:hi - lo], q_part[t % 2][0][rows, half * QH:(half + 1) * QH],
                                     k_part[t % 2][0][rows, lo:hi], start=True, stop=True).then_inc(made["max"], 1)
                elif kind == "shift":
                    reached(pe, max_negated, count(b, "shift", t, u[2]))
                    nc.tensor.matmul(out[SHIFT:STK, 0:QH], neg_max[:, u[2], :], ident[0:QH, 0:QH],
                                     start=True, stop=True).then_inc(made["shift"], 1)
                elif kind == "score":
                    p, j = u[2], u[3]
                    if p == 0 and j == 0:
                        reached(pe, stacked[t % 2], stack_count(b, t))
                        reached(pe, low_stacked, low_count(b, t))
                        reached(pe, shift_copied, count(b, "shift", t, 1))
                    reached(pe, exp_done, count(b, "score", t, p, j) - 2)
                    for k in range(2):
                        kt = 2 * p + k
                        last = nc.tensor.matmul(score_bank[j % 2][:, k * SQ:(k + 1) * SQ],
                                                kstack[t % 2][0:STK, j, kt * KW:kt * KW + P],
                                                qstack[t % 2][:, j, :], start=True, stop=True)
                    last.then_inc(made["score"], 1)
                elif kind == "pv":
                    p = u[2]
                    reached(pe, exp_done, count(b, "score", t, p, HG - 1))
                    if p == 0:
                        reached(pe, normalized, count(b, "sum", t - 2))
                        if t % 2 == 0:
                            reached(pe, v_copied, count(b, "v", 0, t // 2, KT - 1))
                    for k in range(2):
                        kt = 2 * p + k
                        for j in range(HG):
                            col = (t % 2) * P + j * DK
                            last = nc.tensor.matmul(pv_bank[t % 2][j * DK:(j + 1) * DK, 0:SQ],
                                                    values[:, t % NG // 2, kt, col:col + DK],
                                                    probs[p][:, j, k, :], start=(kt == 0), stop=(kt == KT - 1))
                    last.then_inc(made["pv"], 1)
                elif kind == "sum":
                    reached(pe, summed, 5 * (b * NG + t) + 5)
                    for j in range(HG):
                        last = nc.tensor.matmul(pv_bank[t % 2][j * DK:(j + 1) * DK, SQ:2 * SQ], ones[0:KW, :],
                                                prob_sum[:, j, :], start=True, stop=True)
                    last.then_inc(made["sum"], 1)

        phases(pe, body)

    @block.scalar
    def _(act):
        def body(b, units, proj_last, max_last):
            proj = mx = 0
            for u in units:
                kind, t = u[0], u[1]
                if kind in ("k", "q", "v", "xt", "out"):
                    src = proj_bank[proj % 2]
                    proj += 1
                if kind in ("max", "shift"):
                    mbank = max_bank[mx % 2]
                    mx += 1
                if kind == "score":
                    p, j = u[2], u[3]
                    act.wait_ge(made["score"], count(b, *u))
                    if j == 0:
                        reached(act, made["pv"], count(b, "pv", t - 1, p))
                        reached(act, summed, 5 * (b * NG + t - 1) + 2 * p + 1)
                    nc.scalar.activation(probs[p][:, j, :, :], score_bank[j % 2][0:KW, 0:2 * SQ].rearrange(
                        "p (k q) -> p k q", k=2), ACT.Exp, scale=float(DK) ** -0.5).then_inc(exp_done, 1)
                elif kind == "k":
                    lo, hi = KSPLIT[u[2]], KSPLIT[u[2] + 1]
                    act.wait_ge(made["k"], count(b, *u))
                    if u[2] == 0:
                        reached(act, stacked[t % 2], stack_count(b, t - 2))
                        reached(act, made["max"], count(b, "max", t - 2, 15))
                    nc.scalar.activation(k_part[t % 2][0][:, lo:hi], src[:, 0:hi - lo], ACT.Identity,
                                         bias=biases[:, 1, t % NG:t % NG + 1]).then_inc(hi_done["k"], 1)
                elif kind == "q":
                    act.wait_ge(made["q"], count(b, *u))
                    nc.scalar.activation(q_part[t % 2][0][:, :], src[:, 0:SQ], ACT.Identity,
                                         bias=biases[:, 0, t % NG:t % NG + 1]).then_inc(hi_done["q"], 1)
                elif kind == "v":
                    act.wait_ge(made["v"], count(b, *u))
                    if u[3] % 3 == 0:
                        reached(act, made["pv"], count(b, "pv", NG * (t - 1) + 2 * u[2] + 1, 2))
                    nc.scalar.activation(values[:, u[2], u[3], :], src[0:KW, 0:256], ACT.Copy).then_inc(v_copied, 1)
                elif kind == "xt":
                    act.wait_ge(made["xt"], count(b, *u))
                    reached(act, made["q"], count(b, "q", NG * t - 1))
                    nc.scalar.activation(xt_part[0][:, :, u[2] * QH:(u[2] + 1) * QH],
                                         src[:, 0:KC * QH].rearrange("p (c q) -> p c q", c=KC),
                                         ACT.Copy).then_inc(hi_done["xt"], 1)
                elif kind == "ctx":
                    reached(act, ctx_loaded, 16 * (b + t + 1))
                    if u[2] == 0:
                        reached(act, made["k"], count(b, "k", NG * t - 1, 1))
                        reached(act, made["v"], count(b, "v", t - 1, 1, KT - 1))
                    nc.scalar.activation(ctx_hi[:, u[2], 0:SK], ctx_raw[:, u[2], :], ACT.Copy)\
                        .then_inc(hi_done["ctx"], 1)
                elif kind == "shift":
                    act.wait_ge(made["shift"], count(b, *u))
                    row = mbank[SHIFT:STK, 0:QH].unsqueeze(1).to_broadcast([HG, HG, QH])
                    nc.scalar.activation(qstack[t % 2][SHIFT:STK, :, u[2] * QH:(u[2] + 1) * QH], row,
                                         ACT.Copy).then_inc(shift_copied, 1)
                elif kind == "sum":
                    reached(act, normalized, count(b, "sum", t))
                    if t % NG == 0:
                        reached(act, made["out"], count(b, "out", t // NG - 1, 1))
                    nc.scalar.activation(o_part[0][:, t % NG, :], heads[:, :], ACT.Identity,
                                         bias=biases[:, 2, t % NG:t % NG + 1]).then_inc(hi_done["sum"], 1)

        phases(act, body)

    @block.vector
    def _(dve):
        def body(b, units, proj_last, max_last):
            proj = mx = 0
            where = {}
            for u in units:
                kind, t = u[0], u[1]
                if kind in ("k", "q", "v", "xt", "out"):
                    where[u] = proj_bank[proj % 2]
                    proj += 1
                if kind in ("max", "shift"):
                    mbank = max_bank[mx % 2]
                    mx += 1
                if kind == "max":
                    half, j, kh = u[2] // 8, u[2] % 8 // 2, u[2] % 2
                    dve.wait_ge(made["max"], count(b, *u))
                    nc.vector.tensor_reduce(row_max[:, half, j, kh:kh + 1], mbank[0:QH, 0:KSPLIT[kh + 1] - KSPLIT[kh]],
                                            AX.X, ALU.max).then_inc(max_reduced, 1)
                    if u[2] % 8 == 7:
                        dve.wait_ge(max_reduced, count(b, *u))
                        reached(dve, made["shift"], count(b, "shift", t - 1, half))
                        nc.vector.tensor_reduce(neg_max[:, half, :], row_max[:, half, :, :], AX.X, ALU.max,
                                                negate=True).then_inc(max_negated, 1)
                elif kind == "k_lo":
                    k = ("k", t, u[2])
                    lo, hi = KSPLIT[u[2]], KSPLIT[u[2] + 1]
                    dve.wait_ge(hi_done["k"], count(b, *k))
                    if u[2] == 0:
                        reached(dve, stacked[t % 2], stack_count(b, t - 2))
                        reached(dve, low_stacked, low_count(b, t - 1))
                    nc.vector.scalar_tensor_tensor(k_part[t % 2][1][:, lo:hi], where[k][:, 0:hi - lo],
                                                   biases[:, 1, t % NG:t % NG + 1],
                                                   k_part[t % 2][0][:, lo:hi].bitcast(F32), ALU.add,
                                                   ALU.subtract).then_inc(lo_done["k"], 1)
                elif kind == "q_lo":
                    dve.wait_ge(hi_done["q"], count(b, "q", t))
                    nc.vector.scalar_tensor_tensor(q_part[t % 2][1][:, :], where[("q", t)][:, 0:SQ],
                                                   biases[:, 0, t % NG:t % NG + 1],
                                                   q_part[t % 2][0][:, :].bitcast(F32), ALU.add,
                                                   ALU.subtract).then_inc(lo_done["q"], 1)
                elif kind == "xt_lo":
                    k = ("xt", t, u[2])
                    dve.wait_ge(hi_done["xt"], count(b, *k))
                    part = slice(u[2] * QH, (u[2] + 1) * QH)
                    nc.vector.tensor_tensor(xt_part[1][:, :, part],
                                            where[k][:, 0:KC * QH].rearrange("p (c q) -> p c q", c=KC),
                                            xt_part[0][:, :, part].bitcast(F32), ALU.subtract)\
                        .then_inc(lo_done["xt"], 1)
                elif kind == "ctx":
                    dve.wait_ge(hi_done["ctx"], count(b, *u))
                    nc.vector.tensor_tensor(ctx_lo[:, u[2], 0:SK], ctx_raw[:, u[2], :],
                                            ctx_hi[:, u[2], 0:SK].bitcast(F32), ALU.subtract)\
                        .then_inc(lo_done["ctx"], 1)
                elif kind == "sum":
                    dve.wait_ge(made["sum"], count(b, "sum", t))
                    nc.vector.reciprocal(heads[:, :], pv_bank[t % 2][:, SQ:2 * SQ]).then_inc(inverted, 1)
                    dve.wait_ge(inverted, count(b, "sum", t))
                    nc.vector.tensor_tensor(heads[:, :], pv_bank[t % 2][:, 0:SQ], heads[:, :],
                                            ALU.mult).then_inc(normalized, 1)
                elif kind == "sum_lo":
                    dve.wait_ge(hi_done["sum"], count(b, "sum", t))
                    nc.vector.scalar_tensor_tensor(o_part[1][:, t % NG, :], heads[:, :],
                                                   biases[:, 2, t % NG:t % NG + 1],
                                                   o_part[0][:, t % NG, :].bitcast(F32), ALU.add,
                                                   ALU.subtract).then_inc(lo_done["sum"], 1)
                elif kind == "norm":
                    n = 2 * (b + t) + u[2]
                    reached(dve, x_loaded, 16 * (b + t + 1))
                    nc.vector.bn_stats(stats[:, u[2], :], xn[:, u[2], :]).then_inc(stats_done, 1)
                    dve.wait_ge(stats_done, n + 1)
                    nc.vector.memset(spacer[:, :], 0.0)
                    nc.vector.bn_aggr(mean_var[:, u[2], :], stats[:, u[2], :]).then_inc(var_done, 1)
                elif kind == "ffn_quant":
                    chain = 3 * b + t
                    if u[2] == 1:
                        dve.wait_ge(fw_loaded, 16 * chain + 16)
                    else:
                        dve.wait_ge(fw_steps, QSTEPS * chain + u[2] - 1)
                    part = fw_share[:, :]
                    quantize_step(nc, u[2], part, part, part, (fw_power, fw_share), fw_scales).then_inc(fw_steps, 1)
                elif kind == "norm2":
                    n = 2 * (b + t) + u[2]
                    dve.wait_ge(pow_steps, 2 * n + 2)
                    nc.vector.tensor_scalar(xn[:, u[2], :], xn[:, u[2], :], mean_var[:, u[2], 0:1],
                                            rstd[:, u[2]:u[2] + 1], ALU.subtract, ALU.mult).then_inc(xn_done, 1)
                elif kind == "out":
                    dve.wait_ge(made["out"], count(b, *u))
                    reached(dve, bias_added, 2 * (b + t) + u[2] + 1)
                    nc.vector.tensor_tensor(res[:, u[2], :], where[u][0:QH, :], res[:, u[2], :],
                                            ALU.add).then_inc(x1_done, 1)

        phases(dve, body)

    @block.gpsimd
    def _(pool):
        def body(b, units, proj_last, max_last):
            for u in units:
                kind, t = u[0], u[1]
                if kind == "pv":
                    p = u[2]
                    base = 5 * (b * NG + t)
                    pool.wait_ge(exp_done, count(b, "score", t, p, HG - 1))
                    if p == 0:
                        reached(pool, made["sum"], count(b, "sum", t - 1))
                        nc.gpsimd.tensor_tensor(prob_sum[:, :, :], probs[0][:, :, 0, :], probs[0][:, :, 1, :],
                                                ALU.add).then_inc(summed, 1)
                    else:
                        for k in range(2):
                            pool.wait_ge(summed, base + 2 * p - 1 + k)
                            nc.gpsimd.tensor_tensor(prob_sum[:, :, :], prob_sum[:, :, :], probs[p][:, :, k, :],
                                                    ALU.add).then_inc(summed, 1)
                elif kind == "norm":
                    n = 2 * (b + t) + u[2]
                    pool.wait_ge(var_done, n + 1)
                    nc.gpsimd.tensor_tensor(rstd[:, u[2]:u[2] + 1], mean_var[:, u[2], 1:2], ln_consts[0:QH, 1:2],
                                            ALU.add).then_inc(pow_steps, 1)
                    pool.wait_ge(pow_steps, 2 * n + 1)
                    nc.gpsimd.tensor_tensor(rstd[:, u[2]:u[2] + 1], rstd[:, u[2]:u[2] + 1], ln_consts[0:QH, 0:1],
                                            ALU.pow).then_inc(pow_steps, 1)
                elif kind == "load_res":
                    reached(pool, res_loaded, 16 * (b + t + 1))
                    for h in range(2):
                        nc.gpsimd.tensor_tensor(res[:, h, :], res[:, h, :], bo_rows[:, :], ALU.add)\
                            .then_inc(bias_added, 1)

        phases(pool, body)

    @block.sync
    def _(sp):
        def share_of(weights, m, b):
            return weights[m].rearrange("r c -> (r c)").rearrange("(p b k) -> b p k", p=P, k=share)[
                bass.ds(b, 1), :, :].rearrange("b p k -> (b p) k")

        heads_of = [slice(j * DK, (j + 1) * DK) for j in range(HG)]

        def rows(tensor, b, h=None):
            view = tensor.rearrange("b (h p) d -> b p h d", h=2)
            if h is None:
                return view[bass.ds(b, 1), :, :, :].rearrange("b p h d -> (b p) h d")
            return view[bass.ds(b, 1), :, h, :].rearrange("b p d -> (b p) d")

        def body(b, units, proj_last, max_last):
            for u in units:
                kind, t = u[0], u[1]
                if kind == "ffn_load":
                    reached(sp, fw_stored, 16 * (3 * b + t))
                    sp.dma_start(fw_share[:, :], share_of(ffn_raw, t, b)).then_inc(fw_loaded, 16)
                elif kind == "ffn_store":
                    chain = 3 * b + t
                    sp.wait_ge(fw_steps, QSTEPS * (chain + 1))
                    sp.dma_start(share_of(ffn_quant, t, b), fw_share[:, :]).then_inc(fw_stored, 16)
                elif kind == "load_ctx":
                    reached(sp, lo_done["ctx"], KC * (b + t))
                    sp.dma_start(ctx_raw[:, :, :], dram["ctx"][bass.ds(b + t, 1), :, :, :].rearrange(
                        "b p c s -> (b p) c s")).then_inc(ctx_loaded, 16)
                elif kind == "load_x":
                    reached(sp, made["xt"], 2 * (b + t))
                    sp.dma_start(xn[:, :, :], rows(dram["x"], b + t)).then_inc(x_loaded, 16)
                elif kind == "load_res":
                    reached(sp, x1_stored, 32 * (b + t))
                    sp.dma_start(res[:, :, :], rows(dram["x"], b + t)).then_inc(res_loaded, 16)
                elif kind == "out":
                    reached(sp, x1_done, count(b, *u))
                    sp.dma_start(rows(x1, b + t, u[2]), res[:, u[2], :]).then_inc(x1_stored, 16)
                elif kind == "stack_low":
                    par = t % 2
                    reached(sp, lo_done["q"], count(b, "q", t))
                    reached(sp, made["score"], count(b, "score", t - 2, 2, 3))
                    for j in range(HG):
                        sp.dma_start(kstack[par][2 * DK:3 * DK, j, 0:SK].bitcast(F32), k_low[heads_of[j], :].bitcast(F32))\
                            .then_inc(low_stacked, 16)
                elif kind == "stack":
                    par = t % 2
                    for j in range(HG):
                        for r in range(2):
                            sp.dma_start(kstack[par][heads_of[r], j, 0:SK].bitcast(F32),
                                         k_part[par][0][heads_of[j], :].bitcast(F32)).then_inc(stacked[par], 16)
                        for r, qp in enumerate((0, 1, 0)):
                            sp.dma_start(qstack[par][heads_of[r], j, :].bitcast(F32),
                                         q_part[par][qp][heads_of[j], :].bitcast(F32)).then_inc(stacked[par], 16)

        phases(sp, body)
        sp.wait_ge(x1_stored, 32 * batches)
        sp.wait_ge(fw_stored, 48 * batches)


def quantize_step(nc, n, x, a, out, work, scales):
    width = x.shape[1]
    nb = width // BLK
    amax, scale, inv = (s[:, 0:nb] for s in scales)
    power, t = (w[:, 0:width] for w in work)

    def blocks(ap):
        return ap.rearrange("p (n k) -> p n k", k=BLK)

    def spread(ap):
        return ap.unsqueeze(2).to_broadcast([P, nb, BLK])

    dve = nc.vector
    if n == 1:
        return dve.tensor_reduce(amax, blocks(x), AX.X, ALU.max, apply_absolute_value=True)
    if n == 2:
        return dve.tensor_scalar(scale, amax, 1.0 / 6.0, 1e-12, ALU.mult, ALU.max)
    if n == 3:
        return dve.reciprocal(inv, scale)
    if n == 4:
        return dve.tensor_tensor(blocks(a), blocks(x), spread(inv), ALU.mult)
    if n == 5:
        return dve.tensor_scalar(power.bitcast(U32), a.bitcast(U32), EXP_MASK, None, ALU.bitwise_and)
    if n == 6:
        return dve.tensor_scalar(power, power, 1.0, None, ALU.max)
    if n == 7:
        return dve.scalar_tensor_tensor(power.bitcast(U32), a.bitcast(U32), SIGN_MASK, power.bitcast(U32),
                                        ALU.bitwise_and, ALU.bitwise_or)
    if n == 8:
        return dve.scalar_tensor_tensor(t, power, TIE, a, ALU.mult, ALU.add)
    if n == 9:
        return dve.tensor_scalar(t.bitcast(U32), t.bitcast(U32), KEEP_MASK, None, ALU.bitwise_and)
    if n == 10:
        return dve.scalar_tensor_tensor(t, power, -2.0, t, ALU.mult, ALU.add)
    return dve.tensor_tensor(blocks(out), blocks(t), spread(scale), ALU.mult)


def feed_forward_weights(nc, ctx, ffn_quant, ffn, ident):
    raw = [[ctx.enter_context(nc.sbuf_tensor(f"fw_raw{r}{n}", [P, D], F32)) for n in range(3)] for r in range(2)]
    banks = [ctx.enter_context(nc.psum_tensor(f"fw_bank{n}", [P, D], F32)) for n in range(3)]
    loaded = [[ctx.enter_context(nc.semaphore(f"fw_loaded{r}{n}")) for n in range(3)] for r in range(2)]
    turned = ctx.enter_context(nc.semaphore("fw_turned"))
    hi_done = ctx.enter_context(nc.semaphore("fw_hi_done"))
    lo_done = ctx.enter_context(nc.semaphore("fw_lo_done"))
    block = ctx.enter_context(nc.Block())

    def place(n, part, i):
        if n == 2:
            return ffn[2][part][:, bass.ds(i, 1), :].rearrange("p a (m n) -> p (a m) n", m=KC)
        return ffn[n][part][:, :, bass.ds(i * P, P)]

    def trips(engine, body):
        body(0, 0, 0)
        with engine.Fori(0, FC // 2) as i:
            body(2 * i + 1, 1, i)
            body(2 * i + 2, 0, i + 1)

    @block.sync
    def _(sp):
        views = [ffn_quant[0].rearrange("(i p) k -> i p k", p=P), ffn_quant[1].rearrange("(i p) k -> i p k", p=P),
                 ffn_quant[2].rearrange("(m p) (j k) -> j p m k", p=P, k=P)]

        def body(i, r, earlier):
            for n in range(3):
                reached(sp, turned, 3 * i - 5 + n)
                if n == 2:
                    sp.dma_start(raw[r][2][:, :].rearrange("p (m k) -> p m k", k=P),
                                 views[2][bass.ds(i, 1), :, :, :].rearrange("a p m k -> (a p) m k"))\
                        .then_inc(loaded[r][n], 16)
                else:
                    sp.dma_start(raw[r][n][:, :], views[n][bass.ds(i, 1), :, :].rearrange("a p k -> (a p) k"))\
                        .then_inc(loaded[r][n], 16)
        body(0, 0, 0)
        body(1, 1, 0)
        body(2, 0, 1)
        with sp.Fori(1, FC // 2) as i:
            body(2 * i + 1, 1, i)
            body(2 * i + 2, 0, i + 1)

    @block.tensor
    def _(pe):
        def body(i, r, earlier):
            for n in range(3):
                unit = 3 * i + n
                pe.wait_ge(loaded[r][n], 16 * earlier + 16)
                reached(pe, lo_done, unit - 2)
                for c in range(KC):
                    last = nc.tensor.transpose(banks[n][:, c * P:(c + 1) * P], raw[r][n][:, c * P:(c + 1) * P],
                                               ident[:, :])
                last.then_inc(turned, 1)
        trips(pe, body)

    @block.scalar
    def _(act):
        def body(i, r, earlier):
            for n in range(3):
                act.wait_ge(turned, 3 * i + n + 1)
                nc.scalar.activation(place(n, 0, i), banks[n][:, :].rearrange("p (c k) -> p c k", c=KC),
                                     ACT.Copy).then_inc(hi_done, 1)
        trips(act, body)

    @block.vector
    def _(dve):
        def body(i, r, earlier):
            for n in range(3):
                dve.wait_ge(hi_done, 3 * i + n + 1)
                nc.vector.tensor_tensor(place(n, 1, i), banks[n][:, :].rearrange("p (c k) -> p c k", c=KC),
                                        place(n, 0, i).bitcast(F32), ALU.subtract).then_inc(lo_done, 1)
        trips(dve, body)


def period_units(n, first=None, left=None):
    def has(k):
        return (first is None or first + k >= 0) and (left is None or k < left)

    def quant(*steps):
        return [("quant", n, s, has(-1), has(2)) for s in steps if has(-1) or has(2)]

    def when(k, *units):
        return list(units) if has(k) else []

    return [*when(3, ("load", n + 3)), *when(0, ("gate_up", n, 0)), *quant(1, 2),
            *when(-3, ("store", n - 3)), *quant(3, 4), *when(-1, ("load_res", n - 1)),
            *when(1, ("turn_x", n + 1)), *when(-2, ("turn_h", n - 2, 0, has(1))),
            *when(3, ("norm", n + 3)), *when(0, ("hidden", n, 0), ("gate_up", n, 1)),
            *quant(5), *when(1, ("turn_x_lo", n + 1)), *quant(6), *when(-2, ("turn_h_lo", n - 2, 0)),
            *when(-2, ("turn_h", n - 2, 1, has(1)), ("down", n - 2, 0), ("turn_h", n - 2, 2, has(1))),
            *quant(7), *when(0, ("hidden", n, 1)), *when(-2, ("turn_h_lo", n - 2, 1)),
            *when(3, ("normalize", n + 3)), *when(0, ("gate_up", n, 2)), *quant(8, 9),
            *when(-2, ("turn_h_lo", n - 2, 2)), *quant(10), *when(0, ("hidden", n, 2)),
            *when(-2, ("down", n - 2, 1), ("down", n - 2, 2)), *quant(11)]


def ffn_start_units():
    def quant(n):
        return [("quant", n, s, False, True) for s in range(1, QSTEPS + 1)]

    return [("load", 0), ("load", 1), ("norm", 0), ("normalize", 0), *quant(-2), ("turn_x", 0), ("load", 2),
            ("norm", 1), ("normalize", 1), *quant(-1), ("turn_x_lo", 0), ("norm", 2), ("normalize", 2)]


def feed_forward(nc, ctx, x1, out, ffn, ident, ln_consts, tiles):
    def sb(name, shape, dt=F32):
        return ctx.enter_context(nc.sbuf_tensor(name, shape, dt))

    def bank(name):
        return ctx.enter_context(nc.psum_tensor(name, [P, 512], F32))

    def sem(name):
        return ctx.enter_context(nc.semaphore(name))

    W = F + D
    xn = [sb(f"f_xn{i}", [P, D]) for i in range(2)]
    hidden = sb("f_hidden", [P, W])
    scaled = sb("f_scaled", [P, W])
    work = [sb(f"f_{n}", [P, W]) for n in ("power", "round")]
    scales = [sb(f"f_{n}", [P, W // BLK]) for n in ("amax", "scale", "inv_scale")]
    quantized = sb("f_quantized", [P, W])
    xqt = [[sb(f"f_xqt{i}{h}", [P, KC, P], F32R) for h in range(2)] for i in range(2)]
    hqt = [sb(f"f_hqt{h}", [P, FC, P], F32R) for h in range(2)]
    act_gate = [sb(f"f_act_gate{i}", [P, 512]) for i in range(2)]
    res = [sb(f"f_res{i}", [P, D]) for i in range(2)]
    stats = sb("f_stats", [P, 6])
    mean_var = sb("f_mean_var", [P, 2])
    rstd = sb("f_rstd", [P, 1])
    spacer = sb("f_spacer", [P, 1])

    gate_bank = [bank(f"gate_bank{i}") for i in range(2)]
    up_bank = [bank(f"up_bank{i}") for i in range(2)]
    turn_bank = [bank(f"turn_bank{i}") for i in range(2)]
    down_bank = [bank(f"down_bank{i}") for i in range(2)]

    x_loaded = [sem(f"f_x_loaded{i}") for i in range(2)]
    res_loaded = [sem(f"f_res_loaded{i}") for i in range(2)]
    stored = [sem(f"f_stored{i}") for i in range(2)]
    ln_steps = sem("f_ln_steps")
    pow_steps = sem("f_pow_steps")
    x_normed = sem("f_x_normed")
    q_steps = sem("f_quant_steps")
    x_turned = sem("f_x_turned")
    x_hi = sem("f_x_hi")
    x_lo = sem("f_x_lo")
    gated = sem("f_gate_up_made")
    silu_done = sem("f_silu_done")
    hidden_done = sem("f_hidden_done")
    h_turned = sem("f_h_turned")
    h_hi = sem("f_h_hi")
    h_lo = sem("f_h_lo")
    down_part = sem("f_down_part")
    y_done = sem("f_y_done")

    def phases(engine, body):
        body(0, ffn_start_units())
        for n in range(3):
            body(0, period_units(n, first=n))
        with engine.Fori(1, tiles // 2 - 2) as i:
            body(i, period_units(1) + period_units(2))
        for n in range(1, 6):
            body(tiles // 2 - 2, period_units(n, left=4 - n))
        body(tiles // 2 - 2, [("store", 3)])

    def quant_count(tile, step):
        return QSTEPS * tile + step

    def chunk(c):
        return slice(CH[c], CH[c + 1])

    def by_chunk(ap):
        return ap.rearrange("p (m k) -> p m k", k=P)

    block = ctx.enter_context(nc.Block())

    @block.sync
    def _(sp):
        xs = x1.rearrange("b s d -> (b s) d").rearrange("(n p) d -> n p d", p=P)
        ys = out.rearrange("b s d -> (b s) d").rearrange("(n p) d -> n p d", p=P)

        def body(i, units):
            for kind, n, *_rest in units:
                tile = 2 * i + n
                if kind == "load":
                    reached(sp, x_normed, tile - 1)
                    sp.dma_start(xn[n % 2][:, :], xs[bass.ds(tile, 1), :, :].rearrange("a p d -> (a p) d"))\
                        .then_inc(x_loaded[n % 2], 16)
                elif kind == "load_res":
                    reached(sp, stored[n % 2], 16 * (i + n // 2))
                    sp.dma_start(res[n % 2][:, :], xs[bass.ds(tile, 1), :, :].rearrange("a p d -> (a p) d"))\
                        .then_inc(res_loaded[n % 2], 16)
                elif kind == "store":
                    reached(sp, y_done, tile + 1)
                    sp.dma_start(ys[bass.ds(tile, 1), :, :].rearrange("a p d -> (a p) d"), res[n % 2][:, :])\
                        .then_inc(stored[n % 2], 16)
        phases(sp, body)
        for par in range(2):
            sp.wait_ge(stored[par], 16 * (tiles // 2))

    @block.tensor
    def _(pe):
        def body(i, units):
            for kind, n, *rest in units:
                tile = 2 * i + n
                if kind == "turn_x":
                    reached(pe, q_steps, quant_count(tile, QSTEPS))
                    reached(pe, x_lo, tile)
                    reached(pe, h_lo, 3 * (tile - 4) + 2)
                    for c in range(KC):
                        col = F + c * P
                        last = nc.tensor.transpose(turn_bank[0][:, c * P:(c + 1) * P], quantized[:, col:col + P],
                                                   ident[:, :])
                    last.then_inc(x_turned, 1)
                elif kind == "gate_up":
                    c = rest[0]
                    q = 3 * tile + c
                    par = (3 * n + c) % 2
                    w = CH[c + 1] - CH[c]
                    reached(pe, x_lo, tile + 1)
                    reached(pe, hidden_done, q - 1)
                    for m, banks in ((0, gate_bank), (1, up_bank)):
                        k = 0
                        for kc in range(KC):
                            for xs_, ws in PASSES:
                                last = nc.tensor.matmul(banks[par][:, 0:w], xqt[n % 2][xs_][:, kc, :],
                                                        ffn[m][ws][:, kc, chunk(c)], start=(k == 0), stop=(k == 11))
                                k += 1
                    last.then_inc(gated, 1)
                elif kind == "turn_h":
                    c, after_x = rest
                    q = 3 * tile + c
                    reached(pe, q_steps, quant_count(tile + 3, QSTEPS))
                    reached(pe, h_lo, q - 1 if c else q)
                    if c == 1 and after_x:
                        reached(pe, x_lo, tile + 4)
                    for m in range(CH[c] // P, CH[c + 1] // P):
                        col = m * P - CH[c]
                        last = nc.tensor.transpose(turn_bank[1 - c % 2][:, col:col + P],
                                                   quantized[:, m * P:(m + 1) * P], ident[:, :])
                    last.then_inc(h_turned, 1)
                elif kind == "down":
                    c = rest[0]
                    q = 3 * tile + c
                    reached(pe, h_lo, q + 1)
                    if c == 0:
                        reached(pe, y_done, tile)
                    for m in range(CH[c] // P, CH[c + 1] // P):
                        for k, (hs, ws) in enumerate(PASSES):
                            last = nc.tensor.matmul(down_bank[n % 2][:, :], hqt[hs][:, m, :], ffn[2][ws][:, m, :],
                                                    start=(m == 0 and k == 0), stop=(m == FC - 1 and k == 2))
                    last.then_inc(down_part, 1)
        phases(pe, body)

    @block.scalar
    def _(act):
        def body(i, units):
            for kind, n, *rest in units:
                tile = 2 * i + n
                if kind == "turn_x":
                    act.wait_ge(x_turned, tile + 1)
                    nc.scalar.activation(xqt[n % 2][0][:, :, :], by_chunk(turn_bank[0][:, :]),
                                         ACT.Copy).then_inc(x_hi, 1)
                elif kind == "gate_up":
                    c = rest[0]
                    q = 3 * tile + c
                    par = (3 * n + c) % 2
                    w = CH[c + 1] - CH[c]
                    act.wait_ge(gated, q + 1)
                    reached(act, hidden_done, q - 1)
                    nc.scalar.activation(act_gate[par][:, 0:w], gate_bank[par][:, 0:w],
                                         ACT.Silu).then_inc(silu_done, 1)
                elif kind == "turn_h":
                    c = rest[0]
                    q = 3 * tile + c
                    w = CH[c + 1] - CH[c]
                    act.wait_ge(h_turned, q + 1)
                    reached(act, down_part, q - 2)
                    nc.scalar.activation(hqt[0][:, CH[c] // P:CH[c + 1] // P, :],
                                         by_chunk(turn_bank[1 - c % 2][:, 0:w]), ACT.Copy).then_inc(h_hi, 1)
        phases(act, body)

    @block.gpsimd
    def _(pool):
        def body(i, units):
            for kind, n, *_rest in units:
                tile = 2 * i + n
                if kind == "norm":
                    pool.wait_ge(ln_steps, 2 * tile + 2)
                    nc.gpsimd.tensor_tensor(rstd[:, :], mean_var[:, 1:2], ln_consts[:, 1:2],
                                            ALU.add).then_inc(pow_steps, 1)
                    pool.wait_ge(pow_steps, 2 * tile + 1)
                    nc.gpsimd.tensor_tensor(rstd[:, :], rstd[:, :], ln_consts[:, 0:1],
                                            ALU.pow).then_inc(pow_steps, 1)
        phases(pool, body)

    @block.vector
    def _(dve):
        def body(i, units):
            for kind, n, *rest in units:
                tile = 2 * i + n
                if kind == "norm":
                    dve.wait_ge(x_loaded[n % 2], 16 * (i + n // 2) + 16)
                    nc.vector.bn_stats(stats[:, :], xn[n % 2][:, :]).then_inc(ln_steps, 1)
                    dve.wait_ge(ln_steps, 2 * tile + 1)
                    nc.vector.memset(spacer[:, :], 0.0)
                    nc.vector.bn_aggr(mean_var[:, :], stats[:, :]).then_inc(ln_steps, 1)
                elif kind == "normalize":
                    dve.wait_ge(pow_steps, 2 * tile + 2)
                    nc.vector.tensor_scalar(hidden[:, F:W], xn[n % 2][:, :], mean_var[:, 0:1], rstd[:, :],
                                            ALU.subtract, ALU.mult).then_inc(x_normed, 1)
                elif kind == "quant":
                    step, with_h, with_x = rest
                    if step > 1:
                        dve.wait_ge(q_steps, quant_count(tile + 2, step - 1))
                    else:
                        if with_x:
                            reached(dve, x_normed, tile + 3)
                        if with_h:
                            reached(dve, hidden_done, 3 * tile)
                    if step == QSTEPS and with_x:
                        reached(dve, x_turned, tile + 2)
                    if step == QSTEPS and with_h:
                        reached(dve, h_turned, 3 * (tile - 1))
                    cols = slice(0 if with_h else F, W if with_x else F)
                    blks = slice(cols.start // BLK, cols.stop // BLK)
                    quantize_step(nc, step, hidden[:, cols], scaled[:, cols], quantized[:, cols],
                                  [w[:, cols] for w in work], [s[:, blks] for s in scales]).then_inc(q_steps, 1)
                elif kind == "turn_x_lo":
                    dve.wait_ge(x_hi, tile + 1)
                    nc.vector.tensor_tensor(xqt[n % 2][1][:, :, :], by_chunk(turn_bank[0][:, :]),
                                            xqt[n % 2][0][:, :, :].bitcast(F32), ALU.subtract).then_inc(x_lo, 1)
                elif kind == "hidden":
                    c = rest[0]
                    par = (3 * n + c) % 2
                    w = CH[c + 1] - CH[c]
                    dve.wait_ge(silu_done, 3 * tile + c + 1)
                    if c == 0:
                        dve.wait_ge(q_steps, quant_count(tile + 2, 4))
                    nc.vector.tensor_tensor(hidden[:, chunk(c)], act_gate[par][:, 0:w], up_bank[par][:, 0:w],
                                            ALU.mult).then_inc(hidden_done, 1)
                elif kind == "turn_h_lo":
                    c = rest[0]
                    w = CH[c + 1] - CH[c]
                    part = slice(CH[c] // P, CH[c + 1] // P)
                    dve.wait_ge(h_hi, 3 * tile + c + 1)
                    nc.vector.tensor_tensor(hqt[1][:, part, :], by_chunk(turn_bank[1 - c % 2][:, 0:w]),
                                            hqt[0][:, part, :].bitcast(F32), ALU.subtract).then_inc(h_lo, 1)
                elif kind == "store":
                    dve.wait_ge(down_part, 3 * tile + 3)
                    dve.wait_ge(res_loaded[n % 2], 16 * (i + n // 2) + 16)
                    nc.vector.tensor_tensor(res[n % 2][:, :], down_bank[n % 2][:, :], res[n % 2][:, :],
                                            ALU.add).then_inc(y_done, 1)
        phases(dve, body)


def cross_attention_ffn(nc, dram, out):
    batches = dram["x"].shape[0]
    x1 = nc.dram_tensor("x1_scratch", (batches, SQ, D), F32, kind="Internal").ap()
    ffn_raw = [dram[n] for n in ("gate", "up", "down")]
    ffn_quant = [nc.dram_tensor(f"ffn_quant{n}", w.shape, F32, kind="Internal").ap() for n, w in enumerate(ffn_raw)]
    with ExitStack() as whole:
        def keep(name, shape, dt=F32, stack=whole):
            return stack.enter_context(nc.sbuf_tensor(name, shape, dt))

        ident = keep("ident", [P, P])
        ln_consts = keep("ln_consts", [P, 2])
        with ExitStack() as first_half:
            w_hi_lo = [[keep(f"w{n}_{h}", [P, KC, D], F32R, first_half) for h in ("hi", "lo")]
                       for n in ("q", "k", "v", "o")]
            consts = ([keep(f"kstack{i}", [STK, HG, SKP], F32R, first_half) for i in range(2)],
                      keep("ctx_hi", [P, KC, SKP], F32R, first_half),
                      keep("ctx_lo", [P, KC, SKP], F32R, first_half), ident,
                      keep("ones", [P, DK], F32, first_half), ln_consts,
                      keep("biases", [P, 3, KC], F32, first_half), keep("bo_rows", [QH, D], F32, first_half))
            with ExitStack() as ctx:
                attention_weights(nc, ctx, dram, w_hi_lo, consts)
            with ExitStack() as ctx:
                attention(nc, ctx, dram, w_hi_lo, consts, x1, ffn_raw, ffn_quant, batches)
        ffn = [[keep(f"ffn_{n}_{h}", [P, KC, F] if n != "down" else [P, FC, D], F32R) for h in ("hi", "lo")]
               for n in ("gate", "up", "down")]
        with ExitStack() as ctx:
            feed_forward_weights(nc, ctx, ffn_quant, ffn, ident)
        with ExitStack() as ctx:
            feed_forward(nc, ctx, x1, out, ffn, ident, ln_consts, batches * SQ // P)


def kernel(x, ctx_1024, L0_xattn_Wq, L0_xattn_bq, L0_xattn_Wk, L0_xattn_bk, L0_xattn_Wv, L0_xattn_bv,
           L0_xattn_Wo, L0_xattn_bo, L0_ffn_w_gate, L0_ffn_w_up, L0_ffn_w_down):
    import numpy as np
    import concourse.bacc as bacc
    from concourse.bass_utils import run_bass_kernel_spmd

    nc = bacc.Bacc("TRN2", target_bir_lowering=False, num_devices=1)
    batches = x.shape[0]

    def turned(w):
        return np.ascontiguousarray(np.asarray(w).T.reshape(KC, P, D).transpose(1, 0, 2))

    def columns(b):
        return np.ascontiguousarray(np.asarray(b).reshape(KC, P).T)

    arrays = {
        "x": np.ascontiguousarray(x),
        "ctx": np.ascontiguousarray(np.asarray(ctx_1024).reshape(batches, SK, KC, P).transpose(0, 3, 2, 1)),
        "wq": turned(L0_xattn_Wq), "wk": turned(L0_xattn_Wk), "wv": turned(L0_xattn_Wv), "wo": turned(L0_xattn_Wo),
        "bq": columns(L0_xattn_bq), "bk": columns(L0_xattn_bk), "bv": columns(L0_xattn_bv),
        "bo": np.ascontiguousarray(L0_xattn_bo),
        "gate": np.ascontiguousarray(L0_ffn_w_gate), "up": np.ascontiguousarray(L0_ffn_w_up),
        "down": np.ascontiguousarray(L0_ffn_w_down),
    }
    dram = {n: nc.dram_tensor(f"in_{n}", a.shape, mybir.dt.from_np(a.dtype), kind="ExternalInput").ap()
            for n, a in arrays.items()}
    out = nc.dram_tensor("out_0", x.shape, F32, kind="ExternalOutput").ap()
    cross_attention_ffn(nc, dram, out)
    result = run_bass_kernel_spmd(nc, [{f"in_{n}": a for n, a in arrays.items()}], core_ids=[0])
    return result.results[0]["out_0"]
```

```python
import concourse.bass as bass
from concourse import mybir
from contextlib import ExitStack

F32 = mybir.dt.float32
F32R = mybir.dt.float32r
U32 = mybir.dt.uint32
ALU = mybir.AluOpType
ACT = mybir.ActivationFunctionType
AX = mybir.AxisListType

P = 128
D = 512
KC = D // P
DK = 32
HG = P // DK
NG = D // P
SQ = 224
QH = SQ // 2
SK = 750
KT = 6
KW = SK // KT
SKP = (KT - 1) * KW + P + 1
KSPLIT = (0, 376, SK)
SHIFT = 3 * DK
STK = SHIFT + HG
F = 1408
FC = F // P
CH = (0, 512, 1024, F)
BLK = 16
WU = 2 * FC + FC
EPS = 1e-5
PASSES = ((0, 0), (0, 1), (1, 0))
EXP_MASK = 0x7F800000
SIGN_MASK = 0x80000000
KEEP_MASK = 0xFFE00000
TIE = 2.25 - 2.0 ** -22
QSTEPS = 11


def reached(engine, sem, count):
    if not isinstance(count, int) or count > 0:
        engine.wait_ge(sem, count)


FFN_SLOTS = (0, 1, 3)

PLACES = {
    "max": (0.3, 0.31, 1.3, 2.3, 2.31, 3.3, 4.3, 4.31, 5.3, 6.3, 6.31, 7.3, 8.3, 8.31, 9.3, 10.3),
    "shift": (7.4, 11.4), "pv": (5.1, 9.1), "pv_last": 1.1,
    "sum": 8.1, "inverse": (8.2, 8.25), "heads": 8.28, "heads_hi": 9.2, "sum_lo": 10.2,
    "k": (4.8, 5.8), "k_lo": (5.85, 6.85), "q": 6.8, "q_lo": 7.8, "v": (8.8, 10.8, 11.8),
    "out": (2.6, 3.6), "ctx": (0.6, 1.6, 2.6, 3.6), "xt": (2.7, 3.7), "xt_lo": (3.75, 4.75),
    "norm": (5.6, 6.6), "norm2": (8.6, 9.6), "load": 2.6, "load_res": 6.6, "add_bias": 11.9,
    "ffn_quant": (3.5, 4.5, 4.51, 5.5, 6.5, 7.5, 8.5, 9.5, 10.5, 11.5, 11.51), "ffn_store": 11.6,
}


SLOT_PLACES = (
    {
        "max": (0.15, 0.15, 0.74, 1.46, 1.97, 2.82, 3.42, 4.78, 4.89, 5.54, 6.68, 6.73, 7.87, 7.94, 8.54, 9.17),
        "shift": (5.97, 10.64),
        "pv": (6.66, 11.9),
        "pv_last": 0.15,
        "sum": 3.0,
        "inverse": (3.5, 4.19),
        "heads": 6.14,
        "heads_hi": 8.99,
        "sum_lo": 10.06,
        "k": (3.63, 5.52),
        "k_lo": (5.16, 7.64),
        "q": 7.12,
        "q_lo": 8.11,
        "v": (1.67, 8.17, 9.81),
        "out": (2.6, 3.6),
        "ctx": (0.6, 1.6, 2.6, 3.6),
        "xt": (2.7, 3.7),
        "xt_lo": (3.75, 4.75),
        "norm": (5.6, 6.6),
        "norm2": (8.6, 9.6),
        "load": 2.6,
        "load_res": 6.6,
        "ffn_quant": (3.25, 4.97, 6.08, 6.45, 7.12, 8.21, 8.35, 9.18, 9.62, 10.0, 10.54),
        "ffn_store": 11.6,
    },
    {
        "max": (0.15, 0.15, 0.16, 1.32, 1.7, 3.16, 3.74, 4.78, 5.96, 6.34, 6.53, 7.4, 7.73, 8.98, 9.89, 10.16),
        "shift": (9.31, 11.28),
        "pv": (11.25, 11.9),
        "pv_last": 0.15,
        "sum": 3.38,
        "inverse": (4.4, 6.15),
        "heads": 7.19,
        "heads_hi": 8.39,
        "sum_lo": 9.18,
        "k": (0.56, 4.19),
        "k_lo": (2.65, 5.02),
        "q": 7.37,
        "q_lo": 7.77,
        "v": (6.2, 8.43, 9.5),
        "out": (2.69, 5.34),
        "ctx": (0.6, 1.6, 2.6, 3.6),
        "xt": (2.7, 3.7),
        "xt_lo": (3.75, 4.75),
        "norm": (1.3, 1.43),
        "norm2": (3.13, 10.35),
        "load": 2.6,
        "load_res": 6.6,
        "ffn_quant": (3.81, 4.25, 4.6, 4.7, 5.64, 7.25, 8.05, 8.99, 9.45, 11.45, 11.51),
        "ffn_store": 11.6,
    },
    {
        "max": (0.15, 0.15, 0.15, 1.2, 2.66, 3.78, 5.02, 5.05, 6.07, 6.35, 6.69, 7.96, 8.68, 8.78, 11.38, 11.57),
        "shift": (8.56, 11.9),
        "pv": (4.24, 8.63),
        "pv_last": 1.55,
        "sum": 3.62,
        "inverse": (4.6, 5.13),
        "heads": 8.4,
        "heads_hi": 9.04,
        "sum_lo": 11.12,
        "k": (4.97, 5.09),
        "k_lo": (5.08, 5.19),
        "q": 6.6,
        "q_lo": 10.58,
        "v": (10.93, 11.78, 11.9),
        "out": (2.6, 3.6),
        "ctx": (0.15, 0.15, 1.88, 2.49),
        "xt": (0.38, 3.49),
        "xt_lo": (1.0, 4.04),
        "norm": (5.6, 6.6),
        "norm2": (8.6, 9.6),
        "load": 2.6,
        "load_res": 6.6,
        "ffn_quant": (3.62, 3.73, 3.88, 4.04, 5.72, 8.89, 9.04, 9.14, 9.78, 10.37, 11.36),
        "ffn_store": 11.6,
    },
    {
        "max": (0.15, 0.15, 0.24, 0.56, 2.32, 3.66, 4.33, 5.22, 5.65, 6.5, 6.68, 7.23, 7.93, 8.29, 9.12, 10.25),
        "shift": (8.98, 11.73),
        "pv": (7.05, 11.0),
        "pv_last": 2.53,
        "sum": 3.42,
        "inverse": (4.7, 8.27),
        "heads": 8.52,
        "heads_hi": 10.94,
        "sum_lo": 11.23,
        "k": (0.15, 4.4),
        "k_lo": (2.13, 6.73),
        "q": 6.01,
        "q_lo": 6.86,
        "v": (8.23, 9.03, 11.9),
        "out": (2.6, 3.6),
        "ctx": (0.6, 1.6, 2.6, 3.6),
        "xt": (2.7, 3.7),
        "xt_lo": (3.75, 4.75),
        "norm": (5.6, 6.6),
        "norm2": (8.6, 9.6),
        "load": 2.6,
        "load_res": 6.6,
        "ffn_quant": (3.32, 4.06, 4.41, 4.91, 5.42, 5.7, 8.81, 11.04, 11.26, 11.39, 11.51),
        "ffn_store": 11.6,
    },
)


def slot_units(g, first, last):
    at = PLACES | SLOT_PLACES[g]
    placed = [(float(i), ("score", g, i // 4, i % 4)) for i in range(12)]

    def add(where, *units):
        places = where if isinstance(where, tuple) else (where,)
        placed.extend(zip(places, units))

    ahead = not (last and g == NG - 1)
    if ahead:
        add(0.1, ("stack_low", g + 1))
        add(0.12, ("stack", g + 1))
        add(at["max"], *[("max", g + 1, n) for n in range(16)])
        add(at["shift"], *[("shift", g + 1, n) for n in range(2)])
    add(at["pv"], ("pv", g, 0), ("pv", g, 1))
    if not (first and g == 0):
        add(at["pv_last"], ("pv", g - 1, 2))
        add(at["sum"], ("sum", g - 1))
        add(at["inverse"], ("inverse", g - 1, 0), ("inverse", g - 1, 1))
        add(at["heads"], ("heads", g - 1))
        add(at["heads_hi"], ("heads_hi", g - 1))
        add(at["sum_lo"], ("sum_lo", g - 1))
    if g in FFN_SLOTS:
        m = FFN_SLOTS.index(g)
        add(0.11, ("ffn_load", m))
        add(at["ffn_quant"], *[("ffn_quant", m, n + 1) for n in range(QSTEPS)])
        add(at["ffn_store"], ("ffn_store", m))
    if g == 1 and not first:
        add(at["out"], ("out", -1, 0), ("out", -1, 1))
    if g == 0 and not last:
        add((at["load"],) * 2, ("load_ctx", 1), ("load_x", 1))
    if g == 1 and not last:
        add(at["norm"], ("norm", 1, 0), ("norm", 1, 1))
        add(at["norm2"], ("norm2", 1, 0), ("norm2", 1, 1))
    if g == 2 and not last:
        add(at["ctx"], *[("ctx", 1, c) for c in range(KC)])
        add(at["xt"], ("xt", 1, 0), ("xt", 1, 1))
        add(at["xt_lo"], ("xt_lo", 1, 0), ("xt_lo", 1, 1))
    if g == 3:
        add(at["load_res"], ("load_res", 0))
        add(at["add_bias"], ("add_bias", 0))
    if g < 2 or not last:
        add(at["k"], ("k", g + 2, 0), ("k", g + 2, 1))
        add(at["k_lo"], ("k_lo", g + 2, 0), ("k_lo", g + 2, 1))
        add(at["q"], ("q", g + 2))
        add(at["q_lo"], ("q_lo", g + 2))
        ahead, half = g // 2, 1 - g // 2
        add(at["v"], *[("v", ahead, half, 3 * (g % 2) + n) for n in range(3)])
    return [unit for _, unit in sorted(placed, key=lambda item: item[0])]


def batch_units(first, last):
    return [u for g in range(NG) for u in slot_units(g, first, last)]


def start_units():
    units = [("load_x", 0), ("load_w", 0), ("load_ctx", 0), ("load_w", 1), ("load_w", 2), ("load_w", 3)]
    units += [("norm", 0, 0), ("norm", 0, 1), ("norm2", 0, 0), ("norm2", 0, 1)]
    units += [("split_w", 0)] + [("ctx", 0, c) for c in range(KC)] + [("split_w", 1), ("need_w", 0)]
    units += [("k", 0, 0), ("xt", 0, 0), ("k_lo", 0, 0), ("xt_lo", 0, 0), ("xt", 0, 1), ("k", 0, 1)]
    units += [("xt_lo", 0, 1), ("need_w", 1), ("k_lo", 0, 1), ("q", 0), ("q_lo", 0)]
    units += [("stack_low", 0), ("stack", 0), ("split_w", 2)]
    m = [("max", 0, n) for n in range(16)]
    v = [("v", 0, 0, n) for n in range(KT)]
    units += m[0:2] + [("k", 1, 0)] + m[2:4] + [("k", 1, 1)] + m[4:5] + [("k_lo", 1, 0)] + m[5:6]
    units += [("q", 1), ("k_lo", 1, 1)] + m[6:8] + [("q_lo", 1), ("split_w", 3), ("need_w", 3)]
    units += v[0:1] + m[8:10] + v[1:2] + [("shift", 0, 0)] + m[10:12] + v[2:3] + m[12:14] + v[3:4] + m[14:15]
    return units + v[4:5] + m[15:16] + v[5:6] + [("shift", 0, 1)]


END_UNITS = [("pv", 3, 2), ("sum", 3), ("inverse", 3, 0), ("inverse", 3, 1), ("heads", 3), ("heads_hi", 3), ("sum_lo", 3), ("out", 0, 0), ("out", 0, 1)]


def attention(nc, ctx, dram, ident, ln_consts, x1, ffn_raw, ffn_quant, batches):
    def sb(name, shape, dt=F32):
        return ctx.enter_context(nc.sbuf_tensor(name, shape, dt))

    def bank(name):
        return ctx.enter_context(nc.psum_tensor(name, [P, 512], F32))

    def sem(name):
        return ctx.enter_context(nc.semaphore(name))

    w_hi_lo = [[sb(f"w{n}_{h}", [P, KC, D], F32R) for h in ("hi", "lo")] for n in ("k", "q", "v", "o")]
    W_K, W_Q, W_V, W_O = range(4)
    kstack = [sb(f"kstack{i}", [STK, HG, SKP], F32R) for i in range(2)]
    ctx_hi = sb("ctx_hi", [P, KC, SKP], F32R)
    ctx_lo = sb("ctx_lo", [P, KC, SKP], F32R)
    ones = sb("ones", [P, DK])
    biases = sb("biases", [P, 3, KC])
    bo_rows = sb("bo_rows", [QH, D])
    ctx_raw = sb("ctx_raw", [P, KC, SK])
    ctx_part = (ctx_hi, ctx_lo)
    qstack = [sb(f"qstack{i}", [STK, HG, SQ], F32R) for i in range(2)]
    k_low = sb("k_low", [P, SK], F32R)
    k_part = [[sb(f"k_high{i}", [P, SK], F32R), k_low] for i in range(2)]
    q_part = [[sb(f"q_part{i}{h}", [P, SQ], F32R) for h in range(2)] for i in range(2)]
    values_whole = sb("values", [P, 2, KT, 256])
    values = values_whole[0:KW, :, :, :]
    probs_whole = sb("probs", [P, 3, HG, 2, SQ])
    probs = [probs_whole[0:KW, p, :, :, :] for p in range(3)]
    in_values = values_whole[:, :, :, :].rearrange("p a b c -> p (a b c)")
    in_probs = probs_whole[:, :, :, :, :].rearrange("p a b c d -> p (a b c d)")
    w_raw = [idle[:, n * KC * D:(n + 1) * KC * D].rearrange("p (c d) -> p c d", c=KC)
             for idle, n in ((in_values, 0), (in_probs, 0), (in_probs, 1), (in_values, 0))]
    prob_sum = sb("prob_sum", [KW, HG, SQ])
    heads = sb("heads", [P, SQ])
    o_part = [sb(f"o_part{h}", [P, NG, SQ], F32R) for h in range(2)]
    xn = sb("xn", [QH, 2, D])
    xt_part = [sb(f"xt_part{h}", [P, KC, SQ], F32R) for h in range(2)]
    res = sb("res", [QH, 2, D])
    share = F * D // (P * batches)
    fw_share, fw_power = sb("fw_share", [P, share]), sb("fw_power", [P, share])
    fw_scales = [sb(f"fw_{n}", [P, share // BLK]) for n in ("amax", "scale", "inv_scale")]
    stats = sb("stats", [QH, 2, 6])
    mean_var = sb("mean_var", [QH, 2, 2])
    rstd = sb("rstd", [QH, 2])
    spacer = sb("spacer", [P, 1])
    row_max = sb("row_max", [QH, 2, HG, 2])
    neg_max = sb("neg_max", [QH, 2, HG])

    score_bank = [bank(f"score_bank{i}") for i in range(2)]
    max_bank = [bank(f"max_bank{i}") for i in range(2)]
    proj_bank = [bank(f"proj_bank{i}") for i in range(2)]
    pv_bank = [bank(f"pv_bank{i}") for i in range(2)]

    names = ("score", "max", "shift", "k", "q", "v", "xt", "out", "pv", "sum")
    made = {n: sem(f"{n}_made") for n in names}
    exp_done = sem("exp_done")
    hi_done = {n: sem(f"{n}_hi_done") for n in ("k", "q", "xt", "ctx", "sum")}
    lo_done = {n: sem(f"{n}_lo_done") for n in ("k", "q", "xt", "ctx", "sum")}
    v_copied = sem("v_copied")
    shift_copied = sem("shift_copied")
    max_reduced = sem("max_reduced")
    max_negated = sem("max_negated")
    inverted = sem("sum_inverted")
    normalized = sem("heads_normalized")
    summed = sem("probs_summed")
    stats_done = sem("ln_stats")
    var_done = sem("ln_var")
    pow_steps = sem("ln_pow_steps")
    xn_done = sem("xn_done")
    bias_added = sem("res_bias_added")
    x1_done = sem("x1_done")
    ctx_loaded = sem("ctx_loaded")
    x_loaded = sem("x_loaded")
    res_loaded = sem("res_loaded")
    x1_stored = sem("x1_stored")
    stacked = [sem(f"stacked{i}") for i in range(2)]
    low_stacked = sem("low_stacked")
    fw_loaded = sem("fw_share_loaded")
    small_loaded = sem("small_loaded")
    w_loaded = [sem(f"w_loaded{n}") for n in range(4)]
    w_hi_done = sem("w_hi_done")
    w_lo_done = sem("w_lo_done")
    consts_made = sem("consts_made")
    ident_made = sem("ident_made")
    pads_zeroed = sem("pads_zeroed")
    ones_stacked = sem("ones_stacked")
    fw_steps = sem("fw_quant_steps")
    fw_stored = sem("fw_share_stored")
    STACK_DMAS = 5 * HG

    def index_of(unit, b):
        kind = unit[0]
        if kind == "v":
            return ((b + unit[1]) * 2 + unit[2]) * KT + unit[3]
        per = {"score": 12, "max": 16, "shift": 2, "k": 2, "q": 1, "pv": 3, "sum": 1}
        if kind in per:
            place = unit[2] * 4 + unit[3] if kind == "score" else unit[2] if len(unit) > 2 else 0
            return (b * NG + unit[1]) * per[kind] + place
        return (b + unit[1]) * {"xt": 2, "out": 2, "ctx": KC}[kind] + unit[2]

    def count(b, *unit):
        return index_of(unit, b) + 1

    def stack_count(b, t):
        return (b * (NG // 2) + t // 2 + 1) * 16 * STACK_DMAS

    def low_count(b, t):
        return (b * NG + t + 1) * 16 * HG

    def freed(engine, unit, b):
        kind = unit[0]
        done = {"k": lo_done["k"], "q": lo_done["q"], "xt": lo_done["xt"], "v": v_copied, "out": x1_done,
                "max": max_reduced, "shift": shift_copied}[kind]
        reached(engine, done, count(b, *unit))

    def phases(engine, body):
        body(0, start_units(), [None, None], [None, None])
        v_end = [("v", 0, 0, KT - 2), ("v", 0, 0, KT - 1)]
        m_end = [("max", 0, 15), ("shift", 0, 1)]
        body(0, batch_units(True, False), list(v_end), list(m_end))
        with engine.Fori(1, batches - 1) as b:
            body(b, batch_units(False, False), list(v_end), list(m_end))
        v_last = [("v", 0, 1, KT - 2), ("v", 0, 1, KT - 1)]
        body(batches - 1, batch_units(False, True), list(v_end), list(m_end))
        body(batches - 1, END_UNITS, v_last, [None, None])

    block = ctx.enter_context(nc.Block())

    @block.tensor
    def _(pe):
        def body(b, units, proj_last, max_last):
            proj = mx = 0
            for u in units:
                kind, t = u[0], u[1]
                if kind in ("k", "q", "v", "xt", "out"):
                    out = proj_bank[proj % 2]
                    if proj_last[proj % 2] is not None:
                        freed(pe, proj_last[proj % 2], b)
                    proj_last[proj % 2] = u
                    proj += 1
                if kind in ("max", "shift"):
                    out = max_bank[mx % 2]
                    if max_last[mx % 2] is not None:
                        freed(pe, max_last[mx % 2], b)
                    max_last[mx % 2] = u
                    mx += 1
                if kind == "k":
                    lo, hi = KSPLIT[u[2]], KSPLIT[u[2] + 1]
                    g = t % NG
                    if g == 0 and u[2] == 0:
                        reached(pe, lo_done["ctx"], count(b, "ctx", t // NG, KC - 1))
                    n = 0
                    for c in range(KC):
                        for ws, cs in PASSES:
                            last = nc.tensor.matmul(out[:, 0:hi - lo], w_hi_lo[W_K][ws][:, c, g * P:(g + 1) * P],
                                                    ctx_part[cs][:, c, lo:hi], start=(n == 0), stop=(n == 11))
                            n += 1
                    last.then_inc(made["k"], 1)
                elif kind == "q":
                    g = t % NG
                    if g == 0:
                        reached(pe, lo_done["xt"], count(b, "xt", t // NG, 1))
                    n = 0
                    for c in range(KC):
                        for ws, cs in PASSES:
                            last = nc.tensor.matmul(out[:, 0:SQ], w_hi_lo[W_Q][ws][:, c, g * P:(g + 1) * P],
                                                    xt_part[cs][:, c, :], start=(n == 0), stop=(n == 11))
                            n += 1
                    last.then_inc(made["q"], 1)
                elif kind == "v":
                    half, kt = u[2], u[3]
                    n = 0
                    for c in range(KC):
                        for cs, ws in PASSES:
                            last = nc.tensor.matmul(out[:, 0:256], ctx_part[cs][:, c, kt * KW:kt * KW + P],
                                                    w_hi_lo[W_V][ws][:, c, half * 256:(half + 1) * 256],
                                                    start=(n == 0), stop=(n == 11))
                            n += 1
                    last.then_inc(made["v"], 1)
                elif kind == "xt":
                    reached(pe, xn_done, 2 * (b + t) + u[2] + 1)
                    for c in range(KC):
                        last = nc.tensor.transpose(out[:, c * QH:(c + 1) * QH], xn[:, u[2], c * P:(c + 1) * P],
                                                   ident[0:QH, 0:QH])
                    last.then_inc(made["xt"], 1)
                elif kind == "out":
                    reached(pe, lo_done["sum"], count(b, "sum", NG * t + 3))
                    n = 0
                    for g in range(NG):
                        for os_, ws in PASSES:
                            last = nc.tensor.matmul(out[0:QH, :], o_part[os_][:, g, u[2] * QH:(u[2] + 1) * QH],
                                                    w_hi_lo[W_O][ws][:, g, :], start=(n == 0), stop=(n == 11))
                            n += 1
                    last.then_inc(made["out"], 1)
                elif kind == "max":
                    half, j, kh = u[2] // 8, u[2] % 8 // 2, u[2] % 2
                    if u[2] == 0:
                        reached(pe, hi_done["k"], count(b, "k", t, 1))
                        reached(pe, hi_done["q"], count(b, "q", t))
                    lo, hi = KSPLIT[kh], KSPLIT[kh + 1]
                    rows = slice(j * DK, (j + 1) * DK)
                    nc.tensor.matmul(out[0:QH, 0:hi - lo], q_part[t % 2][0][rows, half * QH:(half + 1) * QH],
                                     k_part[t % 2][0][rows, lo:hi], start=True, stop=True).then_inc(made["max"], 1)
                elif kind == "shift":
                    reached(pe, max_negated, count(b, "shift", t, u[2]))
                    nc.tensor.matmul(out[SHIFT:STK, 0:QH], neg_max[:, u[2], :], ident[0:QH, 0:QH],
                                     start=True, stop=True).then_inc(made["shift"], 1)
                elif kind == "score":
                    p, j = u[2], u[3]
                    if p == 0 and j == 0:
                        reached(pe, stacked[t % 2], stack_count(b, t))
                        reached(pe, low_stacked, low_count(b, t))
                        reached(pe, shift_copied, count(b, "shift", t, 1))
                    reached(pe, exp_done, count(b, "score", t, p, j) - 2)
                    for k in range(2):
                        kt = 2 * p + k
                        last = nc.tensor.matmul(score_bank[j % 2][:, k * SQ:(k + 1) * SQ],
                                                kstack[t % 2][0:STK, j, kt * KW:kt * KW + P],
                                                qstack[t % 2][:, j, :], start=True, stop=True)
                    last.then_inc(made["score"], 1)
                elif kind == "pv":
                    p = u[2]
                    reached(pe, exp_done, count(b, "score", t, p, HG - 1))
                    if p == 0:
                        reached(pe, normalized, count(b, "sum", t - 2))
                        if t % 2 == 0:
                            reached(pe, v_copied, count(b, "v", 0, t // 2, KT - 1))
                    for k in range(2):
                        kt = 2 * p + k
                        for j in range(HG):
                            col = (t % 2) * P + j * DK
                            last = nc.tensor.matmul(pv_bank[t % 2][j * DK:(j + 1) * DK, 0:SQ],
                                                    values[:, t % NG // 2, kt, col:col + DK],
                                                    probs[p][:, j, k, :], start=(kt == 0), stop=(kt == KT - 1))
                    last.then_inc(made["pv"], 1)
                elif kind == "sum":
                    reached(pe, summed, 5 * (b * NG + t) + 5)
                    for j in range(HG):
                        last = nc.tensor.matmul(pv_bank[t % 2][j * DK:(j + 1) * DK, SQ:2 * SQ], ones[0:KW, :],
                                                prob_sum[:, j, :], start=True, stop=True)
                    last.then_inc(made["sum"], 1)
                elif kind == "need_w":
                    pe.wait_ge(w_lo_done, t + 1)

        pe.wait_ge(consts_made, 3)
        pe.wait_ge(ident_made, 2)
        pe.wait_ge(pads_zeroed, 4)
        pe.wait_ge(ones_stacked, 2)
        phases(pe, body)

    @block.scalar
    def _(act):
        def body(b, units, proj_last, max_last):
            proj = mx = 0
            for u in units:
                kind, t = u[0], u[1]
                if kind in ("k", "q", "v", "xt", "out"):
                    src = proj_bank[proj % 2]
                    proj += 1
                if kind in ("max", "shift"):
                    mbank = max_bank[mx % 2]
                    mx += 1
                if kind == "score":
                    p, j = u[2], u[3]
                    act.wait_ge(made["score"], count(b, *u))
                    if j == 0:
                        reached(act, made["pv"], count(b, "pv", t - 1, p))
                        reached(act, summed, 5 * (b * NG + t - 1) + 2 * p + 1)
                    nc.scalar.activation(probs[p][:, j, :, :], score_bank[j % 2][0:KW, 0:2 * SQ].rearrange(
                        "p (k q) -> p k q", k=2), ACT.Exp, scale=float(DK) ** -0.5).then_inc(exp_done, 1)
                elif kind == "k":
                    lo, hi = KSPLIT[u[2]], KSPLIT[u[2] + 1]
                    act.wait_ge(made["k"], count(b, *u))
                    if u[2] == 0:
                        reached(act, stacked[t % 2], stack_count(b, t - 2))
                        reached(act, made["max"], count(b, "max", t - 2, 15))
                    nc.scalar.activation(k_part[t % 2][0][:, lo:hi], src[:, 0:hi - lo], ACT.Identity,
                                         bias=biases[:, 1, t % NG:t % NG + 1]).then_inc(hi_done["k"], 1)
                elif kind == "q":
                    act.wait_ge(made["q"], count(b, *u))
                    nc.scalar.activation(q_part[t % 2][0][:, :], src[:, 0:SQ], ACT.Identity,
                                         bias=biases[:, 0, t % NG:t % NG + 1]).then_inc(hi_done["q"], 1)
                elif kind == "v":
                    act.wait_ge(made["v"], count(b, *u))
                    if u[3] % 3 == 0:
                        reached(act, made["pv"], count(b, "pv", NG * (t - 1) + 2 * u[2] + 1, 2))
                    nc.scalar.activation(values[:, u[2], u[3], :], src[0:KW, 0:256], ACT.Copy).then_inc(v_copied, 1)
                elif kind == "xt":
                    act.wait_ge(made["xt"], count(b, *u))
                    reached(act, made["q"], count(b, "q", NG * t - 1))
                    nc.scalar.activation(xt_part[0][:, :, u[2] * QH:(u[2] + 1) * QH],
                                         src[:, 0:KC * QH].rearrange("p (c q) -> p c q", c=KC),
                                         ACT.Copy).then_inc(hi_done["xt"], 1)
                elif kind == "ctx":
                    reached(act, ctx_loaded, 16 * (b + t + 1))
                    if u[2] == 0:
                        reached(act, made["k"], count(b, "k", NG * t - 1, 1))
                        reached(act, made["v"], count(b, "v", t - 1, 1, KT - 1))
                    nc.scalar.activation(ctx_hi[:, u[2], 0:SK], ctx_raw[:, u[2], :], ACT.Copy)\
                        .then_inc(hi_done["ctx"], 1)
                elif kind == "shift":
                    act.wait_ge(made["shift"], count(b, *u))
                    row = mbank[SHIFT:STK, 0:QH].unsqueeze(1).to_broadcast([HG, HG, QH])
                    nc.scalar.activation(qstack[t % 2][SHIFT:STK, :, u[2] * QH:(u[2] + 1) * QH], row,
                                         ACT.Copy).then_inc(shift_copied, 1)
                elif kind == "heads_hi":
                    reached(act, normalized, count(b, "sum", t))
                    if t % NG == 0:
                        reached(act, made["out"], count(b, "out", t // NG - 1, 1))
                    nc.scalar.activation(o_part[0][:, t % NG, :], heads[:, :], ACT.Identity,
                                         bias=biases[:, 2, t % NG:t % NG + 1]).then_inc(hi_done["sum"], 1)
                elif kind == "split_w":
                    act.wait_ge(w_loaded[t], 16)
                    nc.scalar.activation(w_hi_lo[t][0][:, :, :], w_raw[t], ACT.Copy)\
                        .then_inc(w_hi_done, 1)
                elif kind == "need_w" and t == 3:
                    act.wait_ge(w_lo_done, 4)

        act.wait_ge(ident_made, 2)
        for par in range(2):
            nc.scalar.activation(kstack[par][SHIFT:STK, :, :], ident[SHIFT:STK, SHIFT:STK].unsqueeze(2).to_broadcast(
                [HG, HG, SKP]), ACT.Copy).then_inc(ones_stacked, 1)
        act.wait_ge(small_loaded, 64)
        phases(act, body)

    @block.vector
    def _(dve):
        def body(b, units, proj_last, max_last):
            proj = mx = 0
            where = {}
            for u in units:
                kind, t = u[0], u[1]
                if kind in ("k", "q", "v", "xt", "out"):
                    where[u] = proj_bank[proj % 2]
                    proj += 1
                if kind in ("max", "shift"):
                    mbank = max_bank[mx % 2]
                    mx += 1
                if kind == "max":
                    half, j, kh = u[2] // 8, u[2] % 8 // 2, u[2] % 2
                    dve.wait_ge(made["max"], count(b, *u))
                    nc.vector.tensor_reduce(row_max[:, half, j, kh:kh + 1], mbank[0:QH, 0:KSPLIT[kh + 1] - KSPLIT[kh]],
                                            AX.X, ALU.max).then_inc(max_reduced, 1)
                    if u[2] % 8 == 7:
                        dve.wait_ge(max_reduced, count(b, *u))
                        reached(dve, made["shift"], count(b, "shift", t - 1, half))
                        nc.vector.tensor_reduce(neg_max[:, half, :], row_max[:, half, :, :], AX.X, ALU.max,
                                                negate=True).then_inc(max_negated, 1)
                elif kind == "k_lo":
                    k = ("k", t, u[2])
                    lo, hi = KSPLIT[u[2]], KSPLIT[u[2] + 1]
                    dve.wait_ge(hi_done["k"], count(b, *k))
                    if u[2] == 0:
                        reached(dve, stacked[t % 2], stack_count(b, t - 2))
                        reached(dve, low_stacked, low_count(b, t - 1))
                    nc.vector.scalar_tensor_tensor(k_part[t % 2][1][:, lo:hi], where[k][:, 0:hi - lo],
                                                   biases[:, 1, t % NG:t % NG + 1],
                                                   k_part[t % 2][0][:, lo:hi].bitcast(F32), ALU.add,
                                                   ALU.subtract).then_inc(lo_done["k"], 1)
                elif kind == "q_lo":
                    dve.wait_ge(hi_done["q"], count(b, "q", t))
                    nc.vector.scalar_tensor_tensor(q_part[t % 2][1][:, :], where[("q", t)][:, 0:SQ],
                                                   biases[:, 0, t % NG:t % NG + 1],
                                                   q_part[t % 2][0][:, :].bitcast(F32), ALU.add,
                                                   ALU.subtract).then_inc(lo_done["q"], 1)
                elif kind == "xt_lo":
                    k = ("xt", t, u[2])
                    dve.wait_ge(hi_done["xt"], count(b, *k))
                    part = slice(u[2] * QH, (u[2] + 1) * QH)
                    nc.vector.tensor_tensor(xt_part[1][:, :, part],
                                            where[k][:, 0:KC * QH].rearrange("p (c q) -> p c q", c=KC),
                                            xt_part[0][:, :, part].bitcast(F32), ALU.subtract)\
                        .then_inc(lo_done["xt"], 1)
                elif kind == "ctx":
                    dve.wait_ge(hi_done["ctx"], count(b, *u))
                    nc.vector.tensor_tensor(ctx_lo[:, u[2], 0:SK], ctx_raw[:, u[2], :],
                                            ctx_hi[:, u[2], 0:SK].bitcast(F32), ALU.subtract)\
                        .then_inc(lo_done["ctx"], 1)
                elif kind == "inverse":
                    half = slice(u[2] * QH, (u[2] + 1) * QH)
                    dve.wait_ge(made["sum"], count(b, "sum", t))
                    nc.vector.reciprocal(heads[:, half], pv_bank[t % 2][:, SQ + half.start:SQ + half.stop])\
                        .then_inc(inverted, 1)
                elif kind == "heads":
                    dve.wait_ge(inverted, 2 * count(b, "sum", t))
                    nc.vector.tensor_tensor(heads[:, :], pv_bank[t % 2][:, 0:SQ], heads[:, :],
                                            ALU.mult).then_inc(normalized, 1)
                elif kind == "sum_lo":
                    dve.wait_ge(hi_done["sum"], count(b, "sum", t))
                    nc.vector.scalar_tensor_tensor(o_part[1][:, t % NG, :], heads[:, :],
                                                   biases[:, 2, t % NG:t % NG + 1],
                                                   o_part[0][:, t % NG, :].bitcast(F32), ALU.add,
                                                   ALU.subtract).then_inc(lo_done["sum"], 1)
                elif kind == "norm":
                    n = 2 * (b + t) + u[2]
                    reached(dve, x_loaded, 16 * (b + t + 1))
                    nc.vector.bn_stats(stats[:, u[2], :], xn[:, u[2], :]).then_inc(stats_done, 1)
                    dve.wait_ge(stats_done, n + 1)
                    nc.vector.memset(spacer[:, :], 0.0)
                    nc.vector.bn_aggr(mean_var[:, u[2], :], stats[:, u[2], :]).then_inc(var_done, 1)
                elif kind == "ffn_quant":
                    chain = 3 * b + t
                    if u[2] == 1:
                        dve.wait_ge(fw_loaded, 16 * chain + 16)
                    else:
                        dve.wait_ge(fw_steps, QSTEPS * chain + u[2] - 1)
                    part = fw_share[:, :]
                    quantize_step(nc, u[2], part, part, part, (fw_power, fw_share), fw_scales).then_inc(fw_steps, 1)
                elif kind == "norm2":
                    n = 2 * (b + t) + u[2]
                    dve.wait_ge(pow_steps, 2 * n + 2)
                    nc.vector.tensor_scalar(xn[:, u[2], :], xn[:, u[2], :], mean_var[:, u[2], 0:1],
                                            rstd[:, u[2]:u[2] + 1], ALU.subtract, ALU.mult).then_inc(xn_done, 1)
                elif kind == "out":
                    dve.wait_ge(made["out"], count(b, *u))
                    reached(dve, bias_added, 2 * (b + t) + u[2] + 1)
                    nc.vector.tensor_tensor(res[:, u[2], :], where[u][0:QH, :], res[:, u[2], :],
                                            ALU.add).then_inc(x1_done, 1)
                elif kind == "split_w":
                    dve.wait_ge(w_hi_done, t + 1)
                    nc.vector.tensor_tensor(w_hi_lo[t][1][:, :, :], w_raw[t],
                                            w_hi_lo[t][0][:, :, :].bitcast(F32), ALU.subtract).then_inc(w_lo_done, 1)

        nc.vector.memset(ones[:, :], 1.0).then_inc(consts_made, 1)
        nc.vector.memset(ln_consts[:, 0:1], -0.5).then_inc(consts_made, 1)
        nc.vector.memset(ln_consts[:, 1:2], EPS).then_inc(consts_made, 1)
        dve.wait_ge(small_loaded, 64)
        phases(dve, body)

    @block.gpsimd
    def _(pool):
        def body(b, units, proj_last, max_last):
            for u in units:
                kind, t = u[0], u[1]
                if kind == "pv":
                    p = u[2]
                    base = 5 * (b * NG + t)
                    pool.wait_ge(exp_done, count(b, "score", t, p, HG - 1))
                    if p == 0:
                        reached(pool, made["sum"], count(b, "sum", t - 1))
                        nc.gpsimd.tensor_tensor(prob_sum[:, :, :], probs[0][:, :, 0, :], probs[0][:, :, 1, :],
                                                ALU.add).then_inc(summed, 1)
                    else:
                        for k in range(2):
                            pool.wait_ge(summed, base + 2 * p - 1 + k)
                            nc.gpsimd.tensor_tensor(prob_sum[:, :, :], prob_sum[:, :, :], probs[p][:, :, k, :],
                                                    ALU.add).then_inc(summed, 1)
                elif kind == "norm":
                    n = 2 * (b + t) + u[2]
                    pool.wait_ge(var_done, n + 1)
                    nc.gpsimd.tensor_tensor(rstd[:, u[2]:u[2] + 1], mean_var[:, u[2], 1:2], ln_consts[0:QH, 1:2],
                                            ALU.add).then_inc(pow_steps, 1)
                    pool.wait_ge(pow_steps, 2 * n + 1)
                    nc.gpsimd.tensor_tensor(rstd[:, u[2]:u[2] + 1], rstd[:, u[2]:u[2] + 1], ln_consts[0:QH, 0:1],
                                            ALU.pow).then_inc(pow_steps, 1)
                elif kind == "add_bias":
                    reached(pool, res_loaded, 16 * (b + t + 1))
                    for h in range(2):
                        nc.gpsimd.tensor_tensor(res[:, h, :], res[:, h, :], bo_rows[:, :], ALU.add)\
                            .then_inc(bias_added, 1)

        nc.gpsimd.memset(ident[:, :], 0.0).then_inc(ident_made, 1)
        for par in range(2):
            nc.gpsimd.memset(kstack[par][0:SHIFT, :, SK:SKP].bitcast(F32), 0.0).then_inc(pads_zeroed, 1)
        for part in ctx_part:
            nc.gpsimd.memset(part[:, :, SK:SKP].bitcast(F32), 0.0).then_inc(pads_zeroed, 1)
        pool.wait_ge(ident_made, 1)
        nc.gpsimd.affine_select(out=ident[:, :], in_=ident[:, :], compare_op=ALU.not_equal, fill=1.0,
                                base=0, pattern=[[-1, P]], channel_multiplier=1).then_inc(ident_made, 1)
        pool.wait_ge(consts_made, 3)
        pool.wait_ge(small_loaded, 64)
        phases(pool, body)

    @block.sync
    def _(sp):
        def share_of(weights, m, b):
            return weights[m].rearrange("r c -> (r c)").rearrange("(p b k) -> b p k", p=P, k=share)[
                bass.ds(b, 1), :, :].rearrange("b p k -> (b p) k")

        heads_of = [slice(j * DK, (j + 1) * DK) for j in range(HG)]

        def rows(tensor, b, h=None):
            view = tensor.rearrange("b (h p) d -> b p h d", h=2)
            if h is None:
                return view[bass.ds(b, 1), :, :, :].rearrange("b p h d -> (b p) h d")
            return view[bass.ds(b, 1), :, h, :].rearrange("b p d -> (b p) d")

        def body(b, units, proj_last, max_last):
            for u in units:
                kind, t = u[0], u[1]
                if kind == "load_w":
                    if t == 3:
                        sp.wait_ge(w_lo_done, 1)
                    sp.dma_start(w_raw[t], dram[("wk", "wq", "wv", "wo")[t]])\
                        .then_inc(w_loaded[t], 16)
                    if t == 0:
                        for n, src in enumerate((dram["bq"], dram["bk"], dram["bv"])):
                            sp.dma_start(biases[:, n, :], src).then_inc(small_loaded, 16)
                        sp.dma_start(bo_rows[:, :], dram["bo"].partition_broadcast(QH)).then_inc(small_loaded, 16)
                elif kind == "ffn_load":
                    reached(sp, fw_stored, 16 * (3 * b + t))
                    sp.dma_start(fw_share[:, :], share_of(ffn_raw, t, b)).then_inc(fw_loaded, 16)
                elif kind == "ffn_store":
                    chain = 3 * b + t
                    sp.wait_ge(fw_steps, QSTEPS * (chain + 1))
                    sp.dma_start(share_of(ffn_quant, t, b), fw_share[:, :]).then_inc(fw_stored, 16)
                elif kind == "load_ctx":
                    reached(sp, lo_done["ctx"], KC * (b + t))
                    sp.dma_start(ctx_raw[:, :, :], dram["ctx"][bass.ds(b + t, 1), :, :, :].rearrange(
                        "b p c s -> (b p) c s")).then_inc(ctx_loaded, 16)
                elif kind == "load_x":
                    reached(sp, made["xt"], 2 * (b + t))
                    sp.dma_start(xn[:, :, :], rows(dram["x"], b + t)).then_inc(x_loaded, 16)
                elif kind == "load_res":
                    reached(sp, x1_stored, 32 * (b + t))
                    sp.dma_start(res[:, :, :], rows(dram["x"], b + t)).then_inc(res_loaded, 16)
                elif kind == "out":
                    reached(sp, x1_done, count(b, *u))
                    sp.dma_start(rows(x1, b + t, u[2]), res[:, u[2], :]).then_inc(x1_stored, 16)
                elif kind == "stack_low":
                    par = t % 2
                    reached(sp, lo_done["q"], count(b, "q", t))
                    reached(sp, made["score"], count(b, "score", t - 2, 2, 3))
                    for j in range(HG):
                        sp.dma_start(kstack[par][2 * DK:3 * DK, j, 0:SK].bitcast(F32), k_low[heads_of[j], :].bitcast(F32))\
                            .then_inc(low_stacked, 16)
                elif kind == "stack":
                    par = t % 2
                    for j in range(HG):
                        for r in range(2):
                            sp.dma_start(kstack[par][heads_of[r], j, 0:SK].bitcast(F32),
                                         k_part[par][0][heads_of[j], :].bitcast(F32)).then_inc(stacked[par], 16)
                        for r, qp in enumerate((0, 1, 0)):
                            sp.dma_start(qstack[par][heads_of[r], j, :].bitcast(F32),
                                         q_part[par][qp][heads_of[j], :].bitcast(F32)).then_inc(stacked[par], 16)

        phases(sp, body)
        sp.wait_ge(x1_stored, 32 * batches)
        sp.wait_ge(fw_stored, 48 * batches)


def quantize_step(nc, n, x, a, out, work, scales):
    width = x.shape[1]
    nb = width // BLK
    amax, scale, inv = (s[:, 0:nb] for s in scales)
    power, t = (w[:, 0:width] for w in work)

    def blocks(ap):
        return ap.rearrange("p (n k) -> p n k", k=BLK)

    def spread(ap):
        return ap.unsqueeze(2).to_broadcast([P, nb, BLK])

    dve = nc.vector
    if n == 1:
        return dve.tensor_reduce(amax, blocks(x), AX.X, ALU.max, apply_absolute_value=True)
    if n == 2:
        return dve.tensor_scalar(scale, amax, 1.0 / 6.0, 1e-12, ALU.mult, ALU.max)
    if n == 3:
        return dve.reciprocal(inv, scale)
    if n == 4:
        return dve.tensor_tensor(blocks(a), blocks(x), spread(inv), ALU.mult)
    if n == 5:
        return dve.tensor_scalar(power.bitcast(U32), a.bitcast(U32), EXP_MASK, None, ALU.bitwise_and)
    if n == 6:
        return dve.tensor_scalar(power, power, 1.0, None, ALU.max)
    if n == 7:
        return dve.scalar_tensor_tensor(power.bitcast(U32), a.bitcast(U32), SIGN_MASK, power.bitcast(U32),
                                        ALU.bitwise_and, ALU.bitwise_or)
    if n == 8:
        return dve.scalar_tensor_tensor(t, power, TIE, a, ALU.mult, ALU.add)
    if n == 9:
        return dve.tensor_scalar(t.bitcast(U32), t.bitcast(U32), KEEP_MASK, None, ALU.bitwise_and)
    if n == 10:
        return dve.scalar_tensor_tensor(t, power, -2.0, t, ALU.mult, ALU.add)
    return dve.tensor_tensor(blocks(out), blocks(t), spread(scale), ALU.mult)


def feed_forward_weights(nc, ctx, ffn_quant, ffn, ident):
    raw = [[ctx.enter_context(nc.sbuf_tensor(f"fw_raw{r}{n}", [P, D], F32)) for n in range(3)] for r in range(2)]
    banks = [ctx.enter_context(nc.psum_tensor(f"fw_bank{n}", [P, D], F32)) for n in range(3)]
    loaded = [[ctx.enter_context(nc.semaphore(f"fw_loaded{r}{n}")) for n in range(3)] for r in range(2)]
    turned = ctx.enter_context(nc.semaphore("fw_turned"))
    hi_done = ctx.enter_context(nc.semaphore("fw_hi_done"))
    lo_done = ctx.enter_context(nc.semaphore("fw_lo_done"))
    block = ctx.enter_context(nc.Block())

    def place(n, part, i):
        if n == 2:
            return ffn[2][part][:, bass.ds(i, 1), :].rearrange("p a (m n) -> p (a m) n", m=KC)
        return ffn[n][part][:, :, bass.ds(i * P, P)]

    def trips(engine, body):
        body(0, 0, 0)
        with engine.Fori(0, FC // 2) as i:
            body(2 * i + 1, 1, i)
            body(2 * i + 2, 0, i + 1)

    @block.sync
    def _(sp):
        views = [ffn_quant[0].rearrange("(i p) k -> i p k", p=P), ffn_quant[1].rearrange("(i p) k -> i p k", p=P),
                 ffn_quant[2].rearrange("(m p) (j k) -> j p m k", p=P, k=P)]

        def body(i, r, earlier):
            for n in range(3):
                reached(sp, turned, 3 * i - 5 + n)
                if n == 2:
                    sp.dma_start(raw[r][2][:, :].rearrange("p (m k) -> p m k", k=P),
                                 views[2][bass.ds(i, 1), :, :, :].rearrange("a p m k -> (a p) m k"))\
                        .then_inc(loaded[r][n], 16)
                else:
                    sp.dma_start(raw[r][n][:, :], views[n][bass.ds(i, 1), :, :].rearrange("a p k -> (a p) k"))\
                        .then_inc(loaded[r][n], 16)
        body(0, 0, 0)
        body(1, 1, 0)
        body(2, 0, 1)
        with sp.Fori(1, FC // 2) as i:
            body(2 * i + 1, 1, i)
            body(2 * i + 2, 0, i + 1)

    @block.tensor
    def _(pe):
        def body(i, r, earlier):
            for n in range(3):
                unit = 3 * i + n
                pe.wait_ge(loaded[r][n], 16 * earlier + 16)
                reached(pe, lo_done, unit - 2)
                for c in range(KC):
                    last = nc.tensor.transpose(banks[n][:, c * P:(c + 1) * P], raw[r][n][:, c * P:(c + 1) * P],
                                               ident[:, :])
                last.then_inc(turned, 1)
        trips(pe, body)

    @block.scalar
    def _(act):
        def body(i, r, earlier):
            for n in range(3):
                act.wait_ge(turned, 3 * i + n + 1)
                nc.scalar.activation(place(n, 0, i), banks[n][:, :].rearrange("p (c k) -> p c k", c=KC),
                                     ACT.Copy).then_inc(hi_done, 1)
        trips(act, body)

    @block.vector
    def _(dve):
        def body(i, r, earlier):
            for n in range(3):
                dve.wait_ge(hi_done, 3 * i + n + 1)
                nc.vector.tensor_tensor(place(n, 1, i), banks[n][:, :].rearrange("p (c k) -> p c k", c=KC),
                                        place(n, 0, i).bitcast(F32), ALU.subtract).then_inc(lo_done, 1)
        trips(dve, body)


def period_units(n, first=None, left=None):
    def has(k):
        return (first is None or first + k >= 0) and (left is None or k < left)

    def quant(*steps):
        return [("quant", n, s, has(-1), has(2)) for s in steps if has(-1) or has(2)]

    def when(k, *units):
        return list(units) if has(k) else []

    return [*when(3, ("load", n + 3)), *when(0, ("gate_up", n, 0)), *quant(1, 2),
            *when(-3, ("store", n - 3)), *quant(3, 4), *when(-1, ("load_res", n - 1)),
            *when(1, ("turn_x", n + 1)), *when(-2, ("turn_h", n - 2, 0, has(1))),
            *when(3, ("norm", n + 3)), *when(0, ("hidden", n, 0), ("gate_up", n, 1)),
            *quant(5), *when(1, ("turn_x_lo", n + 1)), *quant(6), *when(-2, ("turn_h_lo", n - 2, 0)),
            *when(-2, ("turn_h", n - 2, 1, has(1)), ("down", n - 2, 0), ("turn_h", n - 2, 2, has(1))),
            *quant(7), *when(0, ("hidden", n, 1)), *when(-2, ("turn_h_lo", n - 2, 1)),
            *when(3, ("normalize", n + 3)), *when(0, ("gate_up", n, 2)), *quant(8, 9),
            *when(-2, ("turn_h_lo", n - 2, 2)), *quant(10), *when(0, ("hidden", n, 2)),
            *when(-2, ("down", n - 2, 1), ("down", n - 2, 2)), *quant(11)]


def ffn_start_units():
    def quant(n):
        return [("quant", n, s, False, True) for s in range(1, QSTEPS + 1)]

    return [("load", 0), ("load", 1), ("norm", 0), ("normalize", 0), *quant(-2), ("turn_x", 0), ("load", 2),
            ("norm", 1), ("normalize", 1), *quant(-1), ("turn_x_lo", 0), ("norm", 2), ("normalize", 2)]


def feed_forward(nc, ctx, x1, out, ffn, ident, ln_consts, tiles):
    def sb(name, shape, dt=F32):
        return ctx.enter_context(nc.sbuf_tensor(name, shape, dt))

    def bank(name):
        return ctx.enter_context(nc.psum_tensor(name, [P, 512], F32))

    def sem(name):
        return ctx.enter_context(nc.semaphore(name))

    W = F + D
    xn = [sb(f"f_xn{i}", [P, D]) for i in range(2)]
    hidden = sb("f_hidden", [P, W])
    scaled = sb("f_scaled", [P, W])
    work = [sb(f"f_{n}", [P, W]) for n in ("power", "round")]
    scales = [sb(f"f_{n}", [P, W // BLK]) for n in ("amax", "scale", "inv_scale")]
    quantized = sb("f_quantized", [P, W])
    xqt = [[sb(f"f_xqt{i}{h}", [P, KC, P], F32R) for h in range(2)] for i in range(2)]
    hqt = [sb(f"f_hqt{h}", [P, FC, P], F32R) for h in range(2)]
    act_gate = [sb(f"f_act_gate{i}", [P, 512]) for i in range(2)]
    res = [sb(f"f_res{i}", [P, D]) for i in range(2)]
    stats = sb("f_stats", [P, 6])
    mean_var = sb("f_mean_var", [P, 2])
    rstd = sb("f_rstd", [P, 1])
    spacer = sb("f_spacer", [P, 1])

    gate_bank = [bank(f"gate_bank{i}") for i in range(2)]
    up_bank = [bank(f"up_bank{i}") for i in range(2)]
    turn_bank = [bank(f"turn_bank{i}") for i in range(2)]
    down_bank = [bank(f"down_bank{i}") for i in range(2)]

    x_loaded = [sem(f"f_x_loaded{i}") for i in range(2)]
    res_loaded = [sem(f"f_res_loaded{i}") for i in range(2)]
    stored = [sem(f"f_stored{i}") for i in range(2)]
    ln_steps = sem("f_ln_steps")
    pow_steps = sem("f_pow_steps")
    x_normed = sem("f_x_normed")
    q_steps = sem("f_quant_steps")
    x_turned = sem("f_x_turned")
    x_hi = sem("f_x_hi")
    x_lo = sem("f_x_lo")
    gated = sem("f_gate_up_made")
    silu_done = sem("f_silu_done")
    hidden_done = sem("f_hidden_done")
    h_turned = sem("f_h_turned")
    h_hi = sem("f_h_hi")
    h_lo = sem("f_h_lo")
    down_part = sem("f_down_part")
    y_done = sem("f_y_done")

    def phases(engine, body):
        body(0, ffn_start_units())
        for n in range(3):
            body(0, period_units(n, first=n))
        with engine.Fori(1, tiles // 2 - 2) as i:
            body(i, period_units(1) + period_units(2))
        for n in range(1, 6):
            body(tiles // 2 - 2, period_units(n, left=4 - n))
        body(tiles // 2 - 2, [("store", 3)])

    def quant_count(tile, step):
        return QSTEPS * tile + step

    def chunk(c):
        return slice(CH[c], CH[c + 1])

    def by_chunk(ap):
        return ap.rearrange("p (m k) -> p m k", k=P)

    block = ctx.enter_context(nc.Block())

    @block.sync
    def _(sp):
        xs = x1.rearrange("b s d -> (b s) d").rearrange("(n p) d -> n p d", p=P)
        ys = out.rearrange("b s d -> (b s) d").rearrange("(n p) d -> n p d", p=P)

        def body(i, units):
            for kind, n, *_rest in units:
                tile = 2 * i + n
                if kind == "load":
                    reached(sp, x_normed, tile - 1)
                    sp.dma_start(xn[n % 2][:, :], xs[bass.ds(tile, 1), :, :].rearrange("a p d -> (a p) d"))\
                        .then_inc(x_loaded[n % 2], 16)
                elif kind == "load_res":
                    reached(sp, stored[n % 2], 16 * (i + n // 2))
                    sp.dma_start(res[n % 2][:, :], xs[bass.ds(tile, 1), :, :].rearrange("a p d -> (a p) d"))\
                        .then_inc(res_loaded[n % 2], 16)
                elif kind == "store":
                    reached(sp, y_done, tile + 1)
                    sp.dma_start(ys[bass.ds(tile, 1), :, :].rearrange("a p d -> (a p) d"), res[n % 2][:, :])\
                        .then_inc(stored[n % 2], 16)
        phases(sp, body)
        for par in range(2):
            sp.wait_ge(stored[par], 16 * (tiles // 2))

    @block.tensor
    def _(pe):
        def body(i, units):
            for kind, n, *rest in units:
                tile = 2 * i + n
                if kind == "turn_x":
                    reached(pe, q_steps, quant_count(tile, QSTEPS))
                    reached(pe, x_lo, tile)
                    reached(pe, h_lo, 3 * (tile - 4) + 2)
                    for c in range(KC):
                        col = F + c * P
                        last = nc.tensor.transpose(turn_bank[0][:, c * P:(c + 1) * P], quantized[:, col:col + P],
                                                   ident[:, :])
                    last.then_inc(x_turned, 1)
                elif kind == "gate_up":
                    c = rest[0]
                    q = 3 * tile + c
                    par = (3 * n + c) % 2
                    w = CH[c + 1] - CH[c]
                    reached(pe, x_lo, tile + 1)
                    reached(pe, hidden_done, q - 1)
                    for m, banks in ((0, gate_bank), (1, up_bank)):
                        k = 0
                        for kc in range(KC):
                            for xs_, ws in PASSES:
                                last = nc.tensor.matmul(banks[par][:, 0:w], xqt[n % 2][xs_][:, kc, :],
                                                        ffn[m][ws][:, kc, chunk(c)], start=(k == 0), stop=(k == 11))
                                k += 1
                    last.then_inc(gated, 1)
                elif kind == "turn_h":
                    c, after_x = rest
                    q = 3 * tile + c
                    reached(pe, q_steps, quant_count(tile + 3, QSTEPS))
                    reached(pe, h_lo, q - 1 if c else q)
                    if c == 1 and after_x:
                        reached(pe, x_lo, tile + 4)
                    for m in range(CH[c] // P, CH[c + 1] // P):
                        col = m * P - CH[c]
                        last = nc.tensor.transpose(turn_bank[1 - c % 2][:, col:col + P],
                                                   quantized[:, m * P:(m + 1) * P], ident[:, :])
                    last.then_inc(h_turned, 1)
                elif kind == "down":
                    c = rest[0]
                    q = 3 * tile + c
                    reached(pe, h_lo, q + 1)
                    if c == 0:
                        reached(pe, y_done, tile)
                    for m in range(CH[c] // P, CH[c + 1] // P):
                        for k, (hs, ws) in enumerate(PASSES):
                            last = nc.tensor.matmul(down_bank[n % 2][:, :], hqt[hs][:, m, :], ffn[2][ws][:, m, :],
                                                    start=(m == 0 and k == 0), stop=(m == FC - 1 and k == 2))
                    last.then_inc(down_part, 1)
        phases(pe, body)

    @block.scalar
    def _(act):
        def body(i, units):
            for kind, n, *rest in units:
                tile = 2 * i + n
                if kind == "turn_x":
                    act.wait_ge(x_turned, tile + 1)
                    nc.scalar.activation(xqt[n % 2][0][:, :, :], by_chunk(turn_bank[0][:, :]),
                                         ACT.Copy).then_inc(x_hi, 1)
                elif kind == "gate_up":
                    c = rest[0]
                    q = 3 * tile + c
                    par = (3 * n + c) % 2
                    w = CH[c + 1] - CH[c]
                    act.wait_ge(gated, q + 1)
                    reached(act, hidden_done, q - 1)
                    nc.scalar.activation(act_gate[par][:, 0:w], gate_bank[par][:, 0:w],
                                         ACT.Silu).then_inc(silu_done, 1)
                elif kind == "turn_h":
                    c = rest[0]
                    q = 3 * tile + c
                    w = CH[c + 1] - CH[c]
                    act.wait_ge(h_turned, q + 1)
                    reached(act, down_part, q - 2)
                    nc.scalar.activation(hqt[0][:, CH[c] // P:CH[c + 1] // P, :],
                                         by_chunk(turn_bank[1 - c % 2][:, 0:w]), ACT.Copy).then_inc(h_hi, 1)
        phases(act, body)

    @block.gpsimd
    def _(pool):
        def body(i, units):
            for kind, n, *_rest in units:
                tile = 2 * i + n
                if kind == "norm":
                    pool.wait_ge(ln_steps, 2 * tile + 2)
                    nc.gpsimd.tensor_tensor(rstd[:, :], mean_var[:, 1:2], ln_consts[:, 1:2],
                                            ALU.add).then_inc(pow_steps, 1)
                    pool.wait_ge(pow_steps, 2 * tile + 1)
                    nc.gpsimd.tensor_tensor(rstd[:, :], rstd[:, :], ln_consts[:, 0:1],
                                            ALU.pow).then_inc(pow_steps, 1)
        phases(pool, body)

    @block.vector
    def _(dve):
        def body(i, units):
            for kind, n, *rest in units:
                tile = 2 * i + n
                if kind == "norm":
                    dve.wait_ge(x_loaded[n % 2], 16 * (i + n // 2) + 16)
                    nc.vector.bn_stats(stats[:, :], xn[n % 2][:, :]).then_inc(ln_steps, 1)
                    dve.wait_ge(ln_steps, 2 * tile + 1)
                    nc.vector.memset(spacer[:, :], 0.0)
                    nc.vector.bn_aggr(mean_var[:, :], stats[:, :]).then_inc(ln_steps, 1)
                elif kind == "normalize":
                    dve.wait_ge(pow_steps, 2 * tile + 2)
                    nc.vector.tensor_scalar(hidden[:, F:W], xn[n % 2][:, :], mean_var[:, 0:1], rstd[:, :],
                                            ALU.subtract, ALU.mult).then_inc(x_normed, 1)
                elif kind == "quant":
                    step, with_h, with_x = rest
                    if step > 1:
                        dve.wait_ge(q_steps, quant_count(tile + 2, step - 1))
                    else:
                        if with_x:
                            reached(dve, x_normed, tile + 3)
                        if with_h:
                            reached(dve, hidden_done, 3 * tile)
                    if step == QSTEPS and with_x:
                        reached(dve, x_turned, tile + 2)
                    if step == QSTEPS and with_h:
                        reached(dve, h_turned, 3 * (tile - 1))
                    cols = slice(0 if with_h else F, W if with_x else F)
                    blks = slice(cols.start // BLK, cols.stop // BLK)
                    quantize_step(nc, step, hidden[:, cols], scaled[:, cols], quantized[:, cols],
                                  [w[:, cols] for w in work], [s[:, blks] for s in scales]).then_inc(q_steps, 1)
                elif kind == "turn_x_lo":
                    dve.wait_ge(x_hi, tile + 1)
                    nc.vector.tensor_tensor(xqt[n % 2][1][:, :, :], by_chunk(turn_bank[0][:, :]),
                                            xqt[n % 2][0][:, :, :].bitcast(F32), ALU.subtract).then_inc(x_lo, 1)
                elif kind == "hidden":
                    c = rest[0]
                    par = (3 * n + c) % 2
                    w = CH[c + 1] - CH[c]
                    dve.wait_ge(silu_done, 3 * tile + c + 1)
                    if c == 0:
                        dve.wait_ge(q_steps, quant_count(tile + 2, 4))
                    nc.vector.tensor_tensor(hidden[:, chunk(c)], act_gate[par][:, 0:w], up_bank[par][:, 0:w],
                                            ALU.mult).then_inc(hidden_done, 1)
                elif kind == "turn_h_lo":
                    c = rest[0]
                    w = CH[c + 1] - CH[c]
                    part = slice(CH[c] // P, CH[c + 1] // P)
                    dve.wait_ge(h_hi, 3 * tile + c + 1)
                    nc.vector.tensor_tensor(hqt[1][:, part, :], by_chunk(turn_bank[1 - c % 2][:, 0:w]),
                                            hqt[0][:, part, :].bitcast(F32), ALU.subtract).then_inc(h_lo, 1)
                elif kind == "store":
                    dve.wait_ge(down_part, 3 * tile + 3)
                    dve.wait_ge(res_loaded[n % 2], 16 * (i + n // 2) + 16)
                    nc.vector.tensor_tensor(res[n % 2][:, :], down_bank[n % 2][:, :], res[n % 2][:, :],
                                            ALU.add).then_inc(y_done, 1)
        phases(dve, body)


def cross_attention_ffn(nc, dram, out):
    batches = dram["x"].shape[0]
    x1 = nc.dram_tensor("x1_scratch", (batches, SQ, D), F32, kind="Internal").ap()
    ffn_raw = [dram[n] for n in ("gate", "up", "down")]
    ffn_quant = [nc.dram_tensor(f"ffn_quant{n}", w.shape, F32, kind="Internal").ap() for n, w in enumerate(ffn_raw)]
    with ExitStack() as whole:
        def keep(name, shape, dt=F32):
            return whole.enter_context(nc.sbuf_tensor(name, shape, dt))

        ident = keep("ident", [P, P])
        ln_consts = keep("ln_consts", [P, 2])
        with ExitStack() as ctx:
            attention(nc, ctx, dram, ident, ln_consts, x1, ffn_raw, ffn_quant, batches)
        ffn = [[keep(f"ffn_{n}_{h}", [P, KC, F] if n != "down" else [P, FC, D], F32R) for h in ("hi", "lo")]
               for n in ("gate", "up", "down")]
        with ExitStack() as ctx:
            feed_forward_weights(nc, ctx, ffn_quant, ffn, ident)
        with ExitStack() as ctx:
            feed_forward(nc, ctx, x1, out, ffn, ident, ln_consts, batches * SQ // P)


def kernel(x, ctx_1024, L0_xattn_Wq, L0_xattn_bq, L0_xattn_Wk, L0_xattn_bk, L0_xattn_Wv, L0_xattn_bv,
           L0_xattn_Wo, L0_xattn_bo, L0_ffn_w_gate, L0_ffn_w_up, L0_ffn_w_down):
    import numpy as np
    import concourse.bacc as bacc
    from concourse.bass_utils import run_bass_kernel_spmd

    nc = bacc.Bacc("TRN2", target_bir_lowering=False, num_devices=1)
    batches = x.shape[0]

    def turned(w):
        return np.ascontiguousarray(np.asarray(w).T.reshape(KC, P, D).transpose(1, 0, 2))

    def columns(b):
        return np.ascontiguousarray(np.asarray(b).reshape(KC, P).T)

    arrays = {
        "x": np.ascontiguousarray(x),
        "ctx": np.ascontiguousarray(np.asarray(ctx_1024).reshape(batches, SK, KC, P).transpose(0, 3, 2, 1)),
        "wq": turned(L0_xattn_Wq), "wk": turned(L0_xattn_Wk), "wv": turned(L0_xattn_Wv), "wo": turned(L0_xattn_Wo),
        "bq": columns(L0_xattn_bq), "bk": columns(L0_xattn_bk), "bv": columns(L0_xattn_bv),
        "bo": np.ascontiguousarray(L0_xattn_bo),
        "gate": np.ascontiguousarray(L0_ffn_w_gate), "up": np.ascontiguousarray(L0_ffn_w_up),
        "down": np.ascontiguousarray(L0_ffn_w_down),
    }
    dram = {n: nc.dram_tensor(f"in_{n}", a.shape, mybir.dt.from_np(a.dtype), kind="ExternalInput").ap()
            for n, a in arrays.items()}
    out = nc.dram_tensor("out_0", x.shape, F32, kind="ExternalOutput").ap()
    cross_attention_ffn(nc, dram, out)
    result = run_bass_kernel_spmd(nc, [{f"in_{n}": a for n, a in arrays.items()}], core_ids=[0])
    return result.results[0]["out_0"]
```
